# Optimizing a Trainium2 kernel written in Bass

```python
import numpy as np
import jax
import jax.numpy as jnp

def _softmax(x, axis=-1):
    return jax.nn.softmax(x, axis=axis)

def _gelu(x):
    return jax.nn.gelu(x, approximate=True)

def _silu(x):
    return jax.nn.silu(x)

def _sigmoid(x):
    return jax.nn.sigmoid(x)

def _layernorm(x, axis=-1, eps=1e-05):
    m = jnp.mean(x, axis=axis, keepdims=True)
    v = jnp.var(x, axis=axis, keepdims=True)
    return (x - m) / jnp.sqrt(v + eps)

def _scatter_add(tgt, idx, src, axis=0):
    return tgt.at[idx].add(src)

def _segment_sum(src, seg, n):
    return jax.ops.segment_sum(src, seg, n)
kernel_name = 'mk_cond_seq_d1_seqx_r4_8a4a62'

def setup_inputs(seed: int=0):
    np.random.seed(seed)
    _w = jnp.asarray

    def _rec_inputs():
        import jax
        import jax.numpy as jnp
        _rk = jax.random.key(seed)
        x = -0.0002928 + 1 * jax.random.normal(jax.random.fold_in(_rk, 1), (16, 256, 256), jnp.float32)
        _lenS = 256 - jax.random.randint(jax.random.fold_in(_rk, 7), (16,), 0, max(1, 256 // 4) + 1, jnp.int32)
        _lenS2 = 256 - jax.random.randint(jax.random.fold_in(_rk, 8), (16,), 0, max(1, 256 // 4) + 1, jnp.int32)
        cond_1024 = 0.000887014 + 1.03683 * jax.random.normal(jax.random.fold_in(_rk, 11), (16, 256), jnp.float32)
        return (x, cond_1024)
    x, cond_1024 = _rec_inputs()

    def _L0_cond_setup():
        import jax, jax.numpy as jnp
        import numpy as np
        B, L, D_MODEL, COND = (2, 512, 256, 256)
        D_STATE, EXPAND = (64, 2)
        D_INNER = EXPAND * D_MODEL
        MLP_H = 2 * D_MODEL
        EPS = 1e-05

        def _adaln(x, c, w, b):
            mod = (c @ w + b)[:, None, :]
            shift, scale, gate = jnp.split(mod, 3, axis=-1)
            mu = jnp.mean(x, axis=-1, keepdims=True)
            var = jnp.var(x, axis=-1, keepdims=True)
            normed = (x - mu) * jax.lax.rsqrt(var + EPS) * (1.0 + scale) + shift
            return (normed, gate)

        def _ssm(h, in_w, xproj_w, dt_bias, A_log, Dskip, out_w):
            xz = h @ in_w
            xs, z = jnp.split(xz, 2, axis=-1)
            xs = jax.nn.silu(xs)
            proj = xs @ xproj_w
            dt = jax.nn.softplus(proj[..., :D_INNER] + dt_bias)
            Bm = proj[..., D_INNER:D_INNER + D_STATE]
            Cm = proj[..., D_INNER + D_STATE:]
            A = -jnp.exp(A_log)

            def step(hst, ins):
                dt_t, B_t, C_t, x_t = ins
                dA = jnp.exp(dt_t[:, :, None] * A)
                hst = hst * dA + (dt_t * x_t)[:, :, None] * B_t[:, None, :]
                y_t = jnp.einsum('bds,bs->bd', hst, C_t)
                return (hst, y_t)
            tm = lambda a: jnp.swapaxes(a, 0, 1)
            h0 = jnp.zeros((h.shape[0], D_INNER, D_STATE), h.dtype)
            _, ys = jax.lax.scan(step, h0, (tm(dt), tm(Bm), tm(Cm), tm(xs)))
            y = jnp.swapaxes(ys, 0, 1) + xs * Dskip
            return y * jax.nn.silu(z) @ out_w
        key = jax.random.key(seed)
        ks = jax.random.split(key, 24)
        p = lambda i, shape, s=0.02: jax.random.normal(ks[i], shape, jnp.float32) * s
        inp = {'x': jax.random.normal(ks[0], (B, L, D_MODEL), jnp.float32), 'c': jax.random.normal(ks[1], (B, COND), jnp.float32), 'adaln_mamba_w': p(2, (COND, 3 * D_MODEL)), 'adaln_mamba_b': jnp.zeros((3 * D_MODEL,), jnp.float32), 'adaln_mlp_w': p(3, (COND, 3 * D_MODEL)), 'adaln_mlp_b': jnp.zeros((3 * D_MODEL,), jnp.float32), 'mlp_w1': p(4, (D_MODEL, MLP_H)), 'mlp_w2': p(5, (D_MODEL, MLP_H)), 'mlp_w3': p(6, (MLP_H, D_MODEL))}
        a_init = jnp.log(jnp.tile(jnp.arange(1, D_STATE + 1, dtype=jnp.float32), (D_INNER, 1)))
        for j, pre in enumerate(['fwd', 'bwd']):
            o = 7 + 6 * j
            inp[f'{pre}_in_w'] = p(o, (D_MODEL, 2 * D_INNER))
            inp[f'{pre}_xproj_w'] = p(o + 1, (D_INNER, D_INNER + 2 * D_STATE))
            inp[f'{pre}_dt_bias'] = jnp.zeros((D_INNER,), jnp.float32)
            inp[f'{pre}_A_log'] = a_init
            inp[f'{pre}_D'] = jnp.ones((D_INNER,), jnp.float32)
            inp[f'{pre}_out_w'] = p(o + 2, (D_INNER, D_MODEL))
        return inp
    _L0_cond_all = _L0_cond_setup()
    _L0_cond_in = {k: v for k, v in _L0_cond_all.items() if k in ('adaln_mamba_w', 'adaln_mamba_b', 'adaln_mlp_w', 'adaln_mlp_b', 'mlp_w1', 'mlp_w2', 'mlp_w3', 'fwd_in_w', 'fwd_xproj_w', 'fwd_dt_bias', 'fwd_A_log', 'fwd_D', 'fwd_out_w', 'bwd_in_w', 'bwd_xproj_w', 'bwd_dt_bias', 'bwd_A_log', 'bwd_D', 'bwd_out_w')}
    del _L0_cond_all
    return {'x': x, 'cond_1024': cond_1024, 'L0_cond_adaln_mamba_w': _L0_cond_in['adaln_mamba_w'], 'L0_cond_adaln_mamba_b': _L0_cond_in['adaln_mamba_b'], 'L0_cond_adaln_mlp_w': _L0_cond_in['adaln_mlp_w'], 'L0_cond_adaln_mlp_b': _L0_cond_in['adaln_mlp_b'], 'L0_cond_mlp_w1': _L0_cond_in['mlp_w1'], 'L0_cond_mlp_w2': _L0_cond_in['mlp_w2'], 'L0_cond_mlp_w3': _L0_cond_in['mlp_w3'], 'L0_cond_fwd_in_w': _L0_cond_in['fwd_in_w'], 'L0_cond_fwd_xproj_w': _L0_cond_in['fwd_xproj_w'], 'L0_cond_fwd_dt_bias': _L0_cond_in['fwd_dt_bias'], 'L0_cond_fwd_A_log': _L0_cond_in['fwd_A_log'], 'L0_cond_fwd_D': _L0_cond_in['fwd_D'], 'L0_cond_fwd_out_w': _L0_cond_in['fwd_out_w'], 'L0_cond_bwd_in_w': _L0_cond_in['bwd_in_w'], 'L0_cond_bwd_xproj_w': _L0_cond_in['bwd_xproj_w'], 'L0_cond_bwd_dt_bias': _L0_cond_in['bwd_dt_bias'], 'L0_cond_bwd_A_log': _L0_cond_in['bwd_A_log'], 'L0_cond_bwd_D': _L0_cond_in['bwd_D'], 'L0_cond_bwd_out_w': _L0_cond_in['bwd_out_w']}

def reference(x, cond_1024, L0_cond_adaln_mamba_w, L0_cond_adaln_mamba_b, L0_cond_adaln_mlp_w, L0_cond_adaln_mlp_b, L0_cond_mlp_w1, L0_cond_mlp_w2, L0_cond_mlp_w3, L0_cond_fwd_in_w, L0_cond_fwd_xproj_w, L0_cond_fwd_dt_bias, L0_cond_fwd_A_log, L0_cond_fwd_D, L0_cond_fwd_out_w, L0_cond_bwd_in_w, L0_cond_bwd_xproj_w, L0_cond_bwd_dt_bias, L0_cond_bwd_A_log, L0_cond_bwd_D, L0_cond_bwd_out_w):
    import jax
    import jax.numpy as jnp

    def _L0_cond_ref(x, c, adaln_mamba_w, adaln_mamba_b, adaln_mlp_w, adaln_mlp_b, mlp_w1, mlp_w2, mlp_w3, fwd_in_w, fwd_xproj_w, fwd_dt_bias, fwd_A_log, fwd_D, fwd_out_w, bwd_in_w, bwd_xproj_w, bwd_dt_bias, bwd_A_log, bwd_D, bwd_out_w):
        import jax, jax.numpy as jnp
        import numpy as np
        B, L, D_MODEL, COND = (2, 512, 256, 256)
        D_STATE, EXPAND = (64, 2)
        D_INNER = EXPAND * D_MODEL
        MLP_H = 2 * D_MODEL
        EPS = 1e-05

        def _adaln(x, c, w, b):
            mod = (c @ w + b)[:, None, :]
            shift, scale, gate = jnp.split(mod, 3, axis=-1)
            mu = jnp.mean(x, axis=-1, keepdims=True)
            var = jnp.var(x, axis=-1, keepdims=True)
            normed = (x - mu) * jax.lax.rsqrt(var + EPS) * (1.0 + scale) + shift
            return (normed, gate)

        def _ssm(h, in_w, xproj_w, dt_bias, A_log, Dskip, out_w):
            xz = h @ in_w
            xs, z = jnp.split(xz, 2, axis=-1)
            xs = jax.nn.silu(xs)
            proj = xs @ xproj_w
            dt = jax.nn.softplus(proj[..., :D_INNER] + dt_bias)
            Bm = proj[..., D_INNER:D_INNER + D_STATE]
            Cm = proj[..., D_INNER + D_STATE:]
            A = -jnp.exp(A_log)

            def step(hst, ins):
                dt_t, B_t, C_t, x_t = ins
                dA = jnp.exp(dt_t[:, :, None] * A)
                hst = hst * dA + (dt_t * x_t)[:, :, None] * B_t[:, None, :]
                y_t = jnp.einsum('bds,bs->bd', hst, C_t)
                return (hst, y_t)
            tm = lambda a: jnp.swapaxes(a, 0, 1)
            h0 = jnp.zeros((h.shape[0], D_INNER, D_STATE), h.dtype)
            _, ys = jax.lax.scan(step, h0, (tm(dt), tm(Bm), tm(Cm), tm(xs)))
            y = jnp.swapaxes(ys, 0, 1) + xs * Dskip
            return y * jax.nn.silu(z) @ out_w
        h, gate = _adaln(x, c, adaln_mamba_w, adaln_mamba_b)
        h_fwd = _ssm(h, fwd_in_w, fwd_xproj_w, fwd_dt_bias, fwd_A_log, fwd_D, fwd_out_w)
        h_bwd = jnp.flip(_ssm(jnp.flip(h, 1), bwd_in_w, bwd_xproj_w, bwd_dt_bias, bwd_A_log, bwd_D, bwd_out_w), 1)
        x = x + gate * (h_fwd + h_bwd)
        h, gate = _adaln(x, c, adaln_mlp_w, adaln_mlp_b)
        mlp_out = jax.nn.silu(h @ mlp_w1) * (h @ mlp_w2) @ mlp_w3
        return x + gate * mlp_out
    x = _L0_cond_ref(x, cond_1024, L0_cond_adaln_mamba_w, L0_cond_adaln_mamba_b, L0_cond_adaln_mlp_w, L0_cond_adaln_mlp_b, L0_cond_mlp_w1, L0_cond_mlp_w2, L0_cond_mlp_w3, L0_cond_fwd_in_w, L0_cond_fwd_xproj_w, L0_cond_fwd_dt_bias, L0_cond_fwd_A_log, L0_cond_fwd_D, L0_cond_fwd_out_w, L0_cond_bwd_in_w, L0_cond_bwd_xproj_w, L0_cond_bwd_dt_bias, L0_cond_bwd_A_log, L0_cond_bwd_D, L0_cond_bwd_out_w)
    return x

_drawn_inputs = setup_inputs


def setup_inputs(seed=0):
    import zlib

    import numpy as np

    out = dict(_drawn_inputs(seed))
    spreads = {'L0_cond_adaln_mamba_b': (0.0, 0.1),
     'L0_cond_adaln_mlp_b': (0.0, 0.1),
     'L0_cond_fwd_dt_bias': (0.0, 0.1),
     'L0_cond_fwd_D': (1.0, 0.2),
     'L0_cond_bwd_dt_bias': (0.0, 0.1),
     'L0_cond_bwd_D': (1.0, 0.2)}
    factors = {}
    for name, (base, spread) in spreads.items():
        noise = np.random.default_rng([zlib.crc32(name.encode()), seed]).standard_normal(out[name].shape)
        drawn = base * np.exp(spread * noise) if base else spread * noise
        out[name] = jnp.asarray(drawn.astype(out[name].dtype))
    for name, factor in factors.items():
        out[name] = (out[name] * factor).astype(out[name].dtype)
    return out
```

```python
import concourse.bass as bass
from concourse import mybir
from contextlib import ExitStack

fp32 = mybir.dt.float32
bf16 = mybir.dt.bfloat16
ALU = mybir.AluOpType
ACT = mybir.ActivationFunctionType

BATCH, SEQ, DM = 16, 256, 256
COND = 256
DI, DS = 512, 64
MLP = 512
EPS = 1e-5
P = 128
CB = 2
CH = BATCH // CB
T = CB * SEQ
TB = T // P
MB = DM // P
CK = COND // P
JB = DI // P
DIRS = 2
PASSES = DIRS * CH
QS, GD = 4, 32
NQ, NG = DS // QS, DI // GD
GJ = P // GD
PW = DI + 2 * DS
SHIFT1, SCALE1, GATE1, SHIFT2, SCALE2, GATE2 = (MB * k for k in range(6))
NMOD = 6 * MB


def hold(sp, count, sem, value):
    sp.wait_ge(sem, value)
    sp.sem_inc(count, 1)


def identity_matrix(pool, tile, made, n):
    pool.memset(tile, 1.0).then_inc(made, 1)
    pool.wait_ge(made, n + 1)
    pool.affine_select(out=tile, in_=tile, compare_op=ALU.is_equal, fill=0.0, base=0,
                       pattern=[[-1, P]], channel_multiplier=1).then_inc(made, 1)


def project_phase(nc, x, cond, w_mod, b_mod, w_in, w_xp, dt_bias, mod, scr):
    ctx = ExitStack()
    with ctx:
        def sb(name, shape, dt=fp32):
            return ctx.enter_context(nc.sbuf_tensor(name, shape, dt))

        def sem(name):
            return ctx.enter_context(nc.semaphore(name))

        ident = sb("a_ident", [P, P])
        win = sb("a_win", [P, DIRS, MB, 2 * DI])
        wxp = sb("a_wxp", [P, DIRS, JB, PW])
        dtb = sb("a_dtb", [P, DIRS, JB])
        wmod = sb("a_wmod", [P, 2, CK, 3 * DM])
        bmod = sb("a_bmod", [P, NMOD])
        condT = sb("a_condT", [P, CK, BATCH])
        modc = sb("a_modc", [P, NMOD, CB])
        xt = sb("a_xt", [P, TB, DM])
        stats = sb("a_stats", [P, TB, 6])
        mv = sb("a_mv", [P, TB, 2])
        rvar = sb("a_rvar", [P, TB])
        rstd = sb("a_rstd", [P, TB])
        xn = sb("a_xn", [P, TB, DM])
        hT = sb("a_hT", [P, DIRS, MB, T])
        xs = sb("a_xs", [P, DIRS, JB, T])
        sz = sb("a_sz", [P, JB, T])
        pre = sb("a_pre", [P, JB, T])
        ey = sb("a_ey", [P, JB, T])
        ln = sb("a_ln", [P, JB, T])
        wy = sb("a_wy", [P, JB, T])
        nd = sb("a_nd", [P, JB, T])
        dt = sb("a_dt", [P, JB, T])
        u = sb("a_u", [P, JB, T])
        bt = sb("a_bt", [P, TB, DS])
        ct = sb("a_ct", [DS, T])
        uT = sb("a_uT", [P, TB, DI])
        bank = [ctx.enter_context(nc.psum_tensor(f"a_bank{n}", [P, T], fp32)) for n in range(8)]

        sp_passed = sem("a_sp_passed")
        made = sem("a_made")
        loaded = sem("a_loaded")
        mod_ps = sem("a_mod_ps")
        mod_done = sem("a_mod_done")
        x_loaded = sem("a_x_loaded")
        order = sem("a_order")
        rvar_done = sem("a_rvar_done")
        rstd_done = sem("a_rstd_done")
        xn_done = sem("a_xn_done")
        hT_done = sem("a_hT_done")
        full = sem("a_full")
        evac = sem("a_evac")
        expln = sem("a_expln")
        dt_done = sem("a_dt_done")
        u_done = sem("a_u_done")
        st = {k: sem("a_stored_" + k) for k in ("xs", "sz", "dt", "bc", "ut")}

        XT, XS0, Z0, DT0, B0, C0 = 0, 2, 6, 10, 14, 15
        XS1, Z1, UT0, DT1, B1, C1, UT1, JOBS = 16, 20, 24, 28, 32, 33, 34, 38
        XS, Z, DT, BJ, CJ, UT = (XS0, XS1), (Z0, Z1), (DT0, DT1), (B0, B1), (C0, C1), (UT0, UT1)
        EV = JOBS - 2

        def job_full(c, n):
            return c * JOBS + (n + 2)

        def job_evac(c, n):
            return c * EV + (n - 1 + EV)

        with nc.Block() as block:
            @block.gpsimd
            def _(pool):
                identity_matrix(pool, ident[:], made, 0)

            @block.sync
            def _(sp):
                for k in range(CK):
                    sp.dma_start(condT[:, k, :], cond[:, k * P:(k + 1) * P].rearrange("b p -> p b"),
                                 allow_slow_non_contiguous=True).then_inc(loaded, 16)
                for m in range(2):
                    sp.dma_start(wmod[:, m, :, :], w_mod[m].rearrange("(k p) n -> p k n", p=P)).then_inc(loaded, 16)
                    sp.dma_start(bmod[:, m * 3 * MB:(m + 1) * 3 * MB],
                                 b_mod[m].rearrange("(k p) -> p k", p=P), allow_slow_non_contiguous=True).then_inc(loaded, 16)
                for d in range(DIRS):
                    sp.dma_start(win[:, d, :, :], w_in[d].rearrange("(k p) n -> p k n", p=P)).then_inc(loaded, 16)
                    sp.dma_start(wxp[:, d, :, :], w_xp[d].rearrange("(k p) n -> p k n", p=P)).then_inc(loaded, 16)
                    sp.dma_start(dtb[:, d, :], dt_bias[d].rearrange("(k p) -> p k", p=P),
                                 allow_slow_non_contiguous=True).then_inc(loaded, 16)
                for k in st:
                    sp.sem_inc(st[k], 16)
                with sp.Fori(0, CH) as c:
                    hold(sp, sp_passed, xn_done, c + 1)
                    sp.dma_start(xt[:, :, :],
                                 x[bass.ds(c * CB, CB), :, :].rearrange("b (h p) m -> p (b h) m", p=P)).then_inc(x_loaded, 16)

                    def put(dst, src, what):
                        sp.dma_start(dst, src).then_inc(st[what], 16)

                    def rows(scratch, d):
                        return scratch[bass.ds(c + d * CH, 1), :, :].rearrange("a (k p) n -> p (a k) n", p=P)

                    def put_x(d):
                        hold(sp, sp_passed, evac, job_evac(c, XS[d] + JB - 1))
                        put(rows(scr["xs"], d), xs[:, d, :, :], "xs")
                        hold(sp, sp_passed, evac, job_evac(c, Z[d] + JB - 1))
                        put(rows(scr["sz"], d), sz[:, :, :], "sz")

                    def put_dt(d):
                        hold(sp, sp_passed, evac, job_evac(c, CJ[d]))
                        put(rows(scr["b"], d), bt[:, :, :], "bc")
                        put(scr["c"][bass.ds(c + d * CH, 1), :, :].rearrange("a s t -> s (a t)"), ct[:, :], "bc")
                        hold(sp, sp_passed, dt_done, c * DIRS + (d + 1))
                        put(rows(scr["dt"], d), dt[:, :, :], "dt")

                    def put_ut(d):
                        hold(sp, sp_passed, evac, job_evac(c, UT[d] + TB - 1))
                        put(rows(scr["ut"], d), uT[:, :, :], "ut")

                    put_x(0)
                    put_dt(0)
                    put_x(1)
                    put_ut(0)
                    put_dt(1)
                    put_ut(1)
                for k in ("xs", "sz", "dt", "ut"):
                    sp.wait_ge(st[k], 16 * (PASSES + 1))
                sp.wait_ge(st["bc"], 16 * (2 * PASSES + 1))

            @block.tensor
            def _(pe):
                pe.sem_inc(full, 1)
                pe.wait_ge(loaded, 16 * (CK + 4 + 3 * DIRS))
                for m in range(2):
                    for n in range(3 * MB):
                        col = (m * 3 * MB + n) * BATCH
                        for k in range(CK):
                            last = nc.tensor.matmul(bank[7][:, col:col + BATCH], wmod[:, m, k, n * P:(n + 1) * P],
                                                    condT[:, k, :], start=(k == 0), stop=(k == CK - 1))
                last.then_inc(mod_ps, 1)
                pe.wait_ge(mod_done, 1)
                pe.wait_ge(made, 2)
                with pe.Fori(0, CH) as c:
                    def free(n):
                        if n in (XT + 8, XT + 9):
                            pe.wait_ge(hT_done, c * 8 + 8)
                        elif n >= 8:
                            pe.wait_ge(evac, job_evac(c, n - 8))
                        else:
                            before = max(k for k in range(JOBS) if k % 8 == n)
                            pe.wait_ge(evac, c * EV + (before - 1))

                    pe.wait_ge(xn_done, c + 2)
                    for k in range(MB):
                        free(XT + k)
                        for t in range(TB):
                            last = nc.tensor.transpose(bank[XT + k][:, t * P:(t + 1) * P],
                                                       xn[:, t, k * P:(k + 1) * P], ident[:])
                        last.then_inc(full, 1)

                    def channels(job, d, weights, src, kk):
                        for j in range(JB):
                            n = job + j
                            free(n)
                            for k in range(kk):
                                last = nc.tensor.matmul(bank[n % 8][:, :], weights(k, j), src(k),
                                                        start=(k == 0), stop=(k == kk - 1))
                            last.then_inc(full, 1)

                    def xz(d):
                        pe.wait_ge(hT_done, c * 8 + (6 + 2 * d))
                        channels(XS[d], d, lambda k, j: win[:, d, k, j * P:(j + 1) * P], lambda k: hT[:, d, k, :], MB)
                        channels(Z[d], d, lambda k, j: win[:, d, k, DI + j * P:DI + (j + 1) * P],
                                 lambda k: hT[:, d, k, :], MB)

                    def dtbc(d):
                        pe.wait_ge(evac, job_evac(c, XS[d] + JB - 1))
                        channels(DT[d], d, lambda k, j: wxp[:, d, k, j * P:(j + 1) * P], lambda k: xs[:, d, k, :], JB)
                        free(BJ[d])
                        for t in range(TB):
                            for k in range(JB):
                                last = nc.tensor.matmul(bank[BJ[d] % 8][:, t * DS:(t + 1) * DS],
                                                        xs[:, d, k, t * P:(t + 1) * P], wxp[:, d, k, DI:DI + DS],
                                                        start=(k == 0), stop=(k == JB - 1))
                        last.then_inc(full, 1)
                        free(CJ[d])
                        for k in range(JB):
                            last = nc.tensor.matmul(bank[CJ[d] % 8][0:DS, :], wxp[:, d, k, DI + DS:PW],
                                                    xs[:, d, k, :], start=(k == 0), stop=(k == JB - 1))
                        last.then_inc(full, 1)

                    def turn_u(d):
                        pe.wait_ge(u_done, c * DIRS + (d + 2))
                        for t in range(TB):
                            n = UT[d] + t
                            free(n)
                            for j in range(JB):
                                last = nc.tensor.transpose(bank[n % 8][:, j * P:(j + 1) * P],
                                                           u[:, j, t * P:(t + 1) * P], ident[:])
                            last.then_inc(full, 1)

                    xz(0)
                    dtbc(0)
                    xz(1)
                    turn_u(0)
                    dtbc(1)
                    turn_u(1)

            @block.scalar
            def _(act):
                act.sem_inc(evac, EV)
                with act.Fori(0, CH) as c:
                    act.wait_ge(rvar_done, c + 1)
                    nc.scalar.activation(rstd[:, :], rvar[:, :], ACT.Sqrt).then_inc(rstd_done, 1)
                    for k in range(MB):
                        act.wait_ge(full, job_full(c, XT + k))
                        for d in range(DIRS):
                            for b in range(CB):
                                src = bank[XT + k][:, b * SEQ:(b + 1) * SEQ]
                                nc.scalar.activation(hT[:, d, k, b * SEQ:(b + 1) * SEQ],
                                                     src if d == 0 else src[:, ::-1], ACT.Identity,
                                                     scale=modc[:, SCALE1 + k, b:b + 1],
                                                     bias=modc[:, SHIFT1 + k, b:b + 1]).then_inc(hT_done, 1)

                    def silu_xz(d):
                        act.wait_ge(st["xs"], (c * DIRS + (d + 1)) * 16)
                        for j in range(JB):
                            act.wait_ge(full, job_full(c, XS[d] + j))
                            nc.scalar.activation(xs[:, d, j, :], bank[(XS[d] + j) % 8][:, :], ACT.Silu).then_inc(evac, 1)
                        act.wait_ge(st["sz"], (c * DIRS + (d + 1)) * 16)
                        for j in range(JB):
                            act.wait_ge(full, job_full(c, Z[d] + j))
                            nc.scalar.activation(sz[:, j, :], bank[(Z[d] + j) % 8][:, :], ACT.Silu).then_inc(evac, 1)

                    def softplus_bc(d):
                        act.wait_ge(u_done, c * DIRS + (d + 1))
                        for j in range(JB):
                            src = bank[(DT[d] + j) % 8][:, :]
                            act.wait_ge(full, job_full(c, DT[d] + j))
                            nc.scalar.activation(pre[:, j, :], src, ACT.Identity, bias=dtb[:, d, j:j + 1])
                            nc.scalar.activation(ey[:, j, :], src, ACT.Abs, bias=dtb[:, d, j:j + 1]).then_inc(evac, 1)
                        act.wait_ge(st["bc"], (c * DIRS + d) * 32 + 16)
                        act.wait_ge(full, job_full(c, BJ[d]))
                        nc.scalar.activation(bt[:, :, :], bank[BJ[d] % 8][:, 0:TB * DS].rearrange("p (t s) -> p t s", t=TB),
                                             ACT.Copy).then_inc(evac, 1)
                        act.wait_ge(full, job_full(c, CJ[d]))
                        nc.scalar.activation(ct[:, :], bank[CJ[d] % 8][0:DS, :], ACT.Copy).then_inc(evac, 1)
                        act.wait_ge(evac, job_evac(c, DT[d] + JB - 1))
                        nc.scalar.activation(ey[:, :, :], ey[:, :, :], ACT.Exp, scale=-1.0).then_inc(expln, 1)
                        act.wait_ge(expln, c * 4 + (2 * d + 1))
                        nc.scalar.activation(ln[:, :, :], ey[:, :, :], ACT.Ln, bias=1.0).then_inc(expln, 1)

                    def copy_ut(d):
                        act.wait_ge(st["ut"], (c * DIRS + (d + 1)) * 16)
                        for t in range(TB):
                            act.wait_ge(full, job_full(c, UT[d] + t))
                            nc.scalar.activation(uT[:, t, :], bank[(UT[d] + t) % 8][:, :], ACT.Copy).then_inc(evac, 1)

                    silu_xz(0)
                    softplus_bc(0)
                    silu_xz(1)
                    copy_ut(0)
                    softplus_bc(1)
                    copy_ut(1)

            @block.vector
            def _(dve):
                dve.sem_inc(xn_done, 1)
                dve.sem_inc(u_done, 1)
                dve.wait_ge(loaded, 16 * (CK + 4 + 3 * DIRS))
                dve.wait_ge(mod_ps, 1)
                for n in range(NMOD):
                    one = 1.0 if n in (SCALE1, SCALE1 + 1, SCALE2, SCALE2 + 1) else 0.0
                    last = nc.vector.tensor_scalar(mod[:, n, :], bank[7][:, n * BATCH:(n + 1) * BATCH],
                                                   bmod[:, n:n + 1], one, ALU.add, ALU.add)
                last.then_inc(mod_done, 1)
                dve.wait_ge(mod_done, 1)
                LINKS = 3 + 2 * 3
                with dve.Fori(0, CH) as c:
                    chain = [0]

                    def link(ins):
                        chain[0] += 1
                        ins.then_inc(order, 1)
                        dve.wait_ge(order, c * LINKS + chain[0])

                    dve.wait_ge(x_loaded, (c + 1) * 16)
                    for t in range(TB):
                        last = nc.vector.bn_stats(stats[:, t, :], xt[:, t, :])
                    link(last)
                    nc.vector.tensor_copy(modc[:, :, :], mod[:, :, bass.ds(c * CB, CB)])
                    for t in range(TB):
                        last = nc.vector.bn_aggr(mv[:, t, :], stats[:, t, :])
                    link(last)
                    link(nc.vector.tensor_scalar(rstd[:, :], mv[:, :, 1], EPS, None, ALU.add))
                    nc.vector.reciprocal(rvar[:, :], rstd[:, :]).then_inc(rvar_done, 1)
                    dve.wait_ge(rstd_done, c + 1)
                    for t in range(TB):
                        last = nc.vector.tensor_scalar(xn[:, t, :], xt[:, t, :], mv[:, t, 0:1], rstd[:, t:t + 1],
                                                       ALU.subtract, ALU.mult)
                    last.then_inc(xn_done, 1)
                    for d in range(DIRS):
                        dve.wait_ge(expln, c * 4 + (2 * d + 2))
                        link(nc.vector.tensor_scalar(wy[:, :, :], ey[:, :, :], 1.0, None, ALU.add))
                        nc.vector.scalar_tensor_tensor(out=nd[:, :, :], in0=wy[:, :, :], scalar=-1.0, in1=ey[:, :, :],
                                                       op0=ALU.add, op1=ALU.subtract)
                        nc.vector.scalar_tensor_tensor(out=ln[:, :, :], in0=pre[:, :, :], scalar=0.0, in1=ln[:, :, :],
                                                       op0=ALU.max, op1=ALU.add)
                        dve.wait_ge(st["dt"], (c * DIRS + (d + 1)) * 16)
                        link(nc.vector.reciprocal(dt[:, :, :], wy[:, :, :]))
                        link(nc.vector.tensor_tensor(nd[:, :, :], nd[:, :, :], dt[:, :, :], ALU.mult))
                        nc.vector.tensor_tensor(dt[:, :, :], ln[:, :, :], nd[:, :, :], ALU.subtract).then_inc(dt_done, 1)
                        dve.wait_ge(dt_done, c * DIRS + (d + 1))
                        dve.wait_ge(full, job_full(c, UT0 + TB - 1) if d else c * JOBS + 1)
                        nc.vector.tensor_tensor(u[:, :, :], dt[:, :, :], xs[:, d, :, :], ALU.mult).then_inc(u_done, 1)
                    assert chain[0] == LINKS


def scan_phase(nc, a_log, d_skip, scr):
    ctx = ExitStack()
    with ctx:
        def sb(name, shape, dt=fp32):
            return ctx.enter_context(nc.sbuf_tensor(name, shape, dt))

        def pb(name):
            return ctx.enter_context(nc.psum_tensor(name, [P, T], fp32))

        def sem(name):
            return ctx.enter_context(nc.semaphore(name))

        NDA = 4
        UPQ = NG
        UPP = NQ * UPQ
        NV, NP = UPQ // 4, UPQ - UPQ // 4
        NPROD = TB * QS
        PROD_AT = {0: 0, 2: 1, 4: 2, 6: 3, 8: 4, 10: 5, 12: 6, 13: 7}

        ident = sb("b_ident", [P, P])
        summer = sb("b_summer", [P, GD])
        zero = sb("b_zero", [P, T], bf16)
        negA = sb("b_negA", [P, DIRS, NG, NQ])
        dskip = sb("b_dskip", [P, DIRS, JB])
        dtr = sb("b_dtr", [P, NG, T])
        uT = sb("b_uT", [P, TB, DI])
        bt = sb("b_bt", [P, TB, DS])
        crep = sb("b_crep", [P, 2, T])
        ub = sb("b_ub", [P, 2, TB, NG, QS, GD])
        dA = sb("b_dA", [P, NDA, CB, SEQ])
        hc = sb("b_hc", [P, NG, T])
        xs = sb("b_xs", [P, JB, T])
        sz = sb("b_sz", [P, JB, T])
        y = [pb(f"b_y{j}") for j in range(JB)]
        inp = [pb("b_in0"), pb("b_in1")]
        inv = [pb("b_in2"), pb("b_in3")]

        sp_passed = sem("b_sp_passed")
        made = sem("b_made")
        loaded = sem("b_loaded")
        a_exp = sem("b_a_exp")
        a_done = sem("b_a_done")
        cleared = sem("b_cleared")
        dt_loaded = sem("b_dt_loaded")
        ut_loaded = sem("b_ut_loaded")
        c_loaded = [sem("b_c_loaded0"), sem("b_c_loaded1")]
        xz_loaded = sem("b_xz_loaded")
        prod_act = sem("b_prod_act")
        prod_dve = sem("b_prod_dve")
        exp_done = sem("b_exp_done")
        turned = sem("b_turned")
        scanned = sem("b_scanned")
        hc_pool = sem("b_hc_pool")
        hc_dve = sem("b_hc_dve")
        summed = sem("b_summed")
        y_read = sem("b_y_read")
        gated = sem("b_gated")
        stored = sem("b_stored")

        def is_v(g):
            return g % 4 == 3

        def p_units():
            return [g for g in range(UPQ) if not is_v(g)]

        def at(U, n):
            return U + n

        with nc.Block() as block:
            @block.sync
            def _(sp):
                for d in range(DIRS):
                    for i in range(QS):
                        sp.dma_start(negA[i * GD:(i + 1) * GD, d, :, :],
                                     a_log[d][:, i * NQ:(i + 1) * NQ].rearrange("(g d) q -> d g q", d=GD)).then_inc(loaded, 16)
                    sp.dma_start(dskip[:, d, :], d_skip[d].rearrange("(k p) -> p k", p=P),
                                 allow_slow_non_contiguous=True).then_inc(loaded, 16)
                with sp.Fori(0, PASSES) as p:
                    def rows(scratch):
                        return scratch[bass.ds(p, 1), :, :].rearrange("a (k p) n -> p (a k) n", p=P)

                    hold(sp, sp_passed, prod_act, p * NQ + 1)
                    hold(sp, sp_passed, prod_dve, p * NQ + 1)
                    sp.dma_start(uT[:, :, :], rows(scr["ut"])).then_inc(ut_loaded, 16)
                    sp.dma_start(bt[:, :, :], rows(scr["b"])).then_inc(ut_loaded, 16)

                    hold(sp, sp_passed, hc_pool, p * NQ * NP + 1)
                    hold(sp, sp_passed, hc_dve, p * NQ * NV + 2)
                    for g in range(NG):
                        hold(sp, sp_passed, exp_done, p * UPP + 1) if g else None
                        for i in range(QS):
                            sp.dma_start(dtr[i * GD:(i + 1) * GD, g, :],
                                         scr["dt"][bass.ds(p, 1), g * GD:(g + 1) * GD, :]
                                         .rearrange("a d t -> (a d) t")).then_inc(dt_loaded, 16)
                        if g == 0:
                            for k in range(2):
                                for i in range(QS):
                                    sp.dma_start(crep[i * GD:(i + 1) * GD, k, :],
                                                 scr["c"][bass.ds(p, 1), i * NQ + k:i * NQ + k + 1, :]
                                                 .rearrange("a s t -> (a s) t").broadcast_to((GD, T))).then_inc(c_loaded[k], 16)
                    hold(sp, sp_passed, gated, p * JB + 1)
                    hold(sp, sp_passed, stored, p * 16 + 16)
                    sp.dma_start(xs[:, :, :], rows(scr["xs"])).then_inc(xz_loaded, 16)
                    sp.dma_start(sz[:, :, :], rows(scr["sz"])).then_inc(xz_loaded, 16)
                    with sp.Fori(1, NQ // 2) as half:
                        q = half * 2
                        for k in range(2):
                            hold(sp, sp_passed, hc_pool, (p * NQ + q) * NP + ((k - 1) * NP + 1))
                            hold(sp, sp_passed, hc_dve, (p * NQ + q) * NV + ((k - 1) * NV + 2))
                            for i in range(QS):
                                sp.dma_start(crep[i * GD:(i + 1) * GD, k, :],
                                             scr["c"][bass.ds(p, 1), bass.ds(q + (i * NQ + k), 1), :]
                                             .rearrange("a s t -> (a s) t").broadcast_to((GD, T))).then_inc(c_loaded[k], 16)
                    hold(sp, sp_passed, gated, (p + 1) * JB + 1)
                    sp.dma_start(rows(scr["g"]), xs[:, :, :]).then_inc(stored, 16)
                sp.wait_ge(stored, 16 * (PASSES + 1))

            @block.gpsimd
            def _(pool):
                identity_matrix(pool, ident[:], made, 0)
                pool.memset(summer[:], 0.0).then_inc(made, 1)
                for i in range(QS):
                    pool.wait_ge(made, 3 + i)
                    pool.affine_select(out=summer[:], in_=summer[:], compare_op=ALU.not_equal, fill=1.0, base=-i * GD,
                                       pattern=[[-1, GD]], channel_multiplier=1).then_inc(made, 1)
                pool.memset(zero[:], 0.0).then_inc(made, 1)
                pool.sem_inc(hc_pool, 1)
                pool.sem_inc(gated, 1)
                pool.sem_inc(stored, 16)

                def quad(p, half, k):
                    U = (p * NQ + half * 2) * UPQ
                    pool.wait_ge(c_loaded[k], (p * (NQ // 2) + half + 1) * (QS * 16))
                    for g in p_units():
                        pool.wait_ge(scanned, U + (k * UPQ + g + 1 + NDA))
                        nc.gpsimd.tensor_tensor(hc[:, g, :], hc[:, g, :], crep[:, k, :], ALU.mult).then_inc(hc_pool, 1)

                with pool.Fori(0, PASSES) as p:
                    with pool.Fori(0, NQ // 2) as half:
                        quad(p, half, 0)
                        quad(p, half, 1)
                    pool.wait_ge(xz_loaded, (p + 1) * 32)
                    for j in range(JB):
                        pool.wait_ge(y_read, p * JB + (j + 1 + JB))
                        nc.gpsimd.tensor_tensor(xs[:, j, :], xs[:, j, :], sz[:, j, :], ALU.mult).then_inc(gated, 1)

            @block.scalar
            def _(act):
                act.sem_inc(exp_done, 1)
                act.sem_inc(prod_act, 1)
                act.wait_ge(loaded, 16 * DIRS * (QS + 1))
                nc.scalar.activation(negA[:, :, :, :], negA[:, :, :, :], ACT.Exp).then_inc(a_exp, 1)
                act.wait_ge(a_done, 1)
                act.wait_ge(cleared, 1)

                def product(n, k, col):
                    t, i = divmod(2 * n, QS)
                    return nc.scalar.activation(ub[:, k, t, :, i, :], uT[:, t, :].rearrange("p (g d) -> p g d", g=NG), ACT.Copy,
                                                scale=bt[:, t, bass.ds(col + i * NQ, 1)] if not isinstance(col, int)
                                                else bt[:, t, col + i * NQ:col + i * NQ + 1])

                def quad(d, p, q, k, nxt):
                    U = (p * NQ + q) * UPQ
                    for g in range(UPQ):
                        act.wait_ge(scanned, U + (k * UPQ + g + 1))
                        nc.scalar.activation(dA[:, g % NDA, :, 1:SEQ],
                                             dtr[:, g, :].rearrange("p (b t) -> p b t", b=CB)[:, :, 1:SEQ], ACT.Exp,
                                             scale=negA[:, bass.ds(d, 1), g, bass.ds(q + k, 1)]
                                             .rearrange("p a q -> p (a q)")).then_inc(exp_done, 1)
                        if nxt and g in PROD_AT:
                            if PROD_AT[g] == 0:
                                act.wait_ge(turned, U + (k * UPQ + 1))
                            last = product(PROD_AT[g], (k + 1) % 2, q + (k + 1))
                            if PROD_AT[g] == NPROD // 2 - 1:
                                last.then_inc(prod_act, 1)

                with act.Fori(0, DIRS) as d:
                    with act.Fori(0, CH) as c:
                        p = d * CH + c
                        act.wait_ge(turned, p * UPP + 1)
                        act.wait_ge(ut_loaded, (p + 1) * 32)
                        for n in range(NPROD // 2):
                            last = product(n, 0, 0)
                        last.then_inc(prod_act, 1)
                        act.wait_ge(dt_loaded, (p + 1) * (16 * NG * QS))
                        with act.Fori(0, NQ // 2 - 1) as half:
                            q = half * 2
                            quad(d, p, q, 0, True)
                            quad(d, p, q, 1, True)
                        quad(d, p, NQ - 2, 0, True)
                        quad(d, p, NQ - 2, 1, False)

            @block.vector
            def _(dve):
                dve.sem_inc(scanned, NDA)
                dve.sem_inc(hc_dve, 2)
                dve.sem_inc(prod_dve, 1)
                dve.sem_inc(y_read, JB)
                nc.vector.memset(dA[:, :, :, :], 0.0).then_inc(cleared, 1)
                dve.wait_ge(a_exp, 1)
                nc.vector.tensor_scalar(negA[:, :, :, :], negA[:, :, :, :], -1.0, None, ALU.mult).then_inc(a_done, 1)
                dve.wait_ge(cleared, 1)

                def product(n, k, col):
                    t, i = divmod(2 * n + 1, QS)
                    return nc.vector.tensor_scalar(ub[:, k, t, :, i, :], uT[:, t, :].rearrange("p (g d) -> p g d", g=NG),
                                                   bt[:, t, bass.ds(col + i * NQ, 1)] if not isinstance(col, int)
                                                   else bt[:, t, col + i * NQ:col + i * NQ + 1], None, ALU.mult)

                def times_c(p, half, k, g):
                    U = (p * NQ + half * 2) * UPQ
                    if g == 3:
                        dve.wait_ge(c_loaded[k], (p * (NQ // 2) + half + 1) * (QS * 16))
                    dve.wait_ge(scanned, U + (k * UPQ + g + 1 + NDA))
                    nc.vector.tensor_tensor(hc[:, g, :], inv[g // 4 % 2][:, :], crep[:, k, :], ALU.mult).then_inc(hc_dve, 1)

                def quad(p, half, k, nxt):
                    q = half * 2
                    U = (p * NQ + q) * UPQ
                    G = (p * NQ + q) * (UPQ // GJ)
                    for g in range(UPQ):
                        dve.wait_ge(exp_done, U + (k * UPQ + g + 1 + 1))
                        dve.wait_ge(turned, U + (k * UPQ + g + 1 + 1))
                        if g % GJ == 0:
                            dve.wait_ge(summed, G + (k * (UPQ // GJ) + g // GJ + 1))
                        if is_v(g):
                            bank = inv[g // 4 % 2][:, :]
                            out = bank
                        else:
                            bank = inp[p_units().index(g) % 2][:, :]
                            out = hc[:, g, :]
                        nc.vector.tensor_tensor_scan(out, dA[:, g % NDA, :, :].rearrange("p b t -> p (b t)"), bank, 0.0,
                                                     ALU.mult, ALU.add).then_inc(scanned, 1)
                        if g and is_v(g - 1):
                            times_c(p, half, k, g - 1)
                        if nxt and g in PROD_AT:
                            if PROD_AT[g] == 0:
                                dve.wait_ge(turned, U + (k * UPQ + 1))
                            last = product(PROD_AT[g], (k + 1) % 2, q + (k + 1))
                            if PROD_AT[g] == NPROD // 2 - 1:
                                last.then_inc(prod_dve, 1)
                    times_c(p, half, k, UPQ - 1)

                with dve.Fori(0, DIRS) as d:
                    with dve.Fori(0, CH) as c:
                        p = d * CH + c
                        dve.wait_ge(turned, p * UPP + 1)
                        dve.wait_ge(ut_loaded, (p + 1) * 32)
                        for n in range(NPROD // 2):
                            last = product(n, 0, 0)
                        last.then_inc(prod_dve, 1)
                        with dve.Fori(0, NQ // 2 - 1) as half:
                            quad(p, half, 0, True)
                            quad(p, half, 1, True)
                        quad(p, NQ // 2 - 1, 0, True)
                        quad(p, NQ // 2 - 1, 1, False)
                        dve.wait_ge(xz_loaded, (p + 1) * 32)
                        for j in range(JB):
                            dve.wait_ge(summed, (p + 1) * (UPP // GJ) - (JB - 1 - j) + 4)
                            nc.vector.scalar_tensor_tensor(out=xs[:, j, :], in0=xs[:, j, :],
                                                           scalar=dskip[:, bass.ds(d, 1), j], in1=y[j][:, :],
                                                           op0=ALU.mult, op1=ALU.add).then_inc(y_read, 1)

            @block.tensor
            def _(pe):
                pe.sem_inc(turned, 1)
                pe.sem_inc(summed, 4)
                pe.wait_ge(made, 3 + QS + 1)

                def turn(p, q, k, j):
                    U = (p * NQ + q) * UPQ + (k * UPQ + j * GJ)
                    V = (p * NQ + q) * NV + (k * NV + j)
                    kk, jj = (k + j // 4) % 2, j % 4
                    if jj == 0:
                        pe.wait_ge(prod_act, (p * NQ + q) + (k + j // 4 + 1 + 1))
                        pe.wait_ge(prod_dve, (p * NQ + q) + (k + j // 4 + 1 + 1))
                    for e in range(GJ):
                        g = jj * GJ + e
                        if is_v(g):
                            pe.wait_ge(hc_dve, V + 1)
                            bank = inv[g // 4 % 2]
                        else:
                            n = p_units().index(g)
                            user = p_units()[n - 2] - (UPQ if n < 2 else 0)
                            pe.wait_ge(scanned, U + (user - jj * GJ + 1 + NDA))
                            bank = inp[n % 2]
                        for t in range(TB):
                            last = nc.tensor.transpose(bank[:, t * P:(t + 1) * P],
                                                       ub[:, kk, t, g, :, :].rearrange("p i d -> p (i d)"), ident[:])
                        last.then_inc(turned, 1)

                def add(p, q, k, j, stop=False):
                    U = (p * NQ + q)
                    pe.wait_ge(hc_pool, U * NP + (k * NP + 3 * (j + 1) + 1))
                    pe.wait_ge(hc_dve, U * NV + (k * NV + j + 1 + 2))
                    for e in range(GJ):
                        last = nc.tensor.matmul(y[j][e * GD:(e + 1) * GD, :], summer[:, :], hc[:, j * GJ + e, :],
                                                start=False, stop=stop, tile_position=(0, e * GD), skip_group_check=True)
                    last.then_inc(summed, 1)

                with pe.Fori(0, PASSES) as p:
                    for j in range(JB):
                        pe.wait_ge(y_read, p * JB + (j + 1))
                        nc.tensor.matmul(y[j][:, :], zero[:, 0:P], zero[:, :], start=True, stop=False,
                                         skip_group_check=True)
                    turn(p, 0, 0, 0)
                    turn(p, 0, 0, 1)
                    with pe.Fori(0, NQ // 2 - 1) as half:
                        q = half * 2
                        for k in range(2):
                            for j in range(4):
                                turn(p, q, k, j + 2)
                                add(p, q, k, j)
                    for k in range(2):
                        for j in range(4):
                            if k == 0 or j < 2:
                                turn(p, NQ - 2, k, j + 2)
                            add(p, NQ - 2, k, j, stop=(k == 1))


def output_phase(nc, x, w_out, w1, w2, w3, mod, scr, out):
    ctx = ExitStack()
    with ctx:
        def sb(name, shape, dt=fp32):
            return ctx.enter_context(nc.sbuf_tensor(name, shape, dt))

        def sem(name):
            return ctx.enter_context(nc.semaphore(name))

        ident = sb("c_ident", [P, P])
        mean_w = sb("c_mean_w", [P, P])
        wo = sb("c_wo", [P, DIRS, JB, DM])
        w1s = sb("c_w1", [P, MB, MLP])
        w2s = sb("c_w2", [P, MB, MLP])
        w3s = sb("c_w3", [P, JB, DM])
        modc = sb("c_modc", [P, NMOD, CB])
        xt = sb("c_xt", [P, TB, DM])
        gs = sb("c_gs", [P, DIRS, JB, T])
        of = sb("c_of", [P, MB, T])
        x1 = sb("c_x1", [P, MB, T])
        xc = sb("c_xc", [P, MB, T])
        sq = sb("c_sq", [P, MB, T])
        ve = sb("c_ve", [P, T])
        rv = sb("c_rv", [P, T])
        rs = sb("c_rs", [P, T])
        xm = sb("c_xm", [P, MB, T])
        h2 = sb("c_h2", [P, MB, T])
        gate = sb("c_gate", [P, JB, T])
        x2 = sb("c_x2", [P, MB, T])
        ot = sb("c_ot", [P, TB, DM])
        bank = [ctx.enter_context(nc.psum_tensor(f"c_bank{n}", [P, T], fp32)) for n in range(8)]
        OF, OB, XT, MEAN, VAR, UP, DOWN, OUT, JOBS = 0, 2, 4, 6, 7, 8, 16, 18, 20

        sp_passed = sem("c_sp_passed")
        made = sem("c_made")
        loaded = sem("c_loaded")
        in_loaded = sem("c_in_loaded")
        full = sem("c_full")
        of_done = sem("c_of_done")
        order = sem("c_order")
        x1_done = sem("c_x1_done")
        xc_done = sem("c_xc_done")
        sq_done = sem("c_sq_done")
        rv_done = sem("c_rv_done")
        rs_done = sem("c_rs_done")
        h2_done = sem("c_h2_done")
        silu_done = sem("c_silu_done")
        gate_done = sem("c_gate_done")
        x2_done = sem("c_x2_done")
        copied = sem("c_copied")
        stored = sem("c_stored")

        def job_full(c, n):
            return c * JOBS + (n + 2)

        NW = DIRS + 3
        with nc.Block() as block:
            @block.gpsimd
            def _(pool):
                identity_matrix(pool, ident[:], made, 0)
                pool.memset(mean_w[:], 1.0 / DM).then_inc(made, 1)

            @block.sync
            def _(sp):
                for d in range(DIRS):
                    sp.dma_start(wo[:, d, :, :], w_out[d].rearrange("(k p) n -> p k n", p=P)).then_inc(loaded, 16)
                for dst, src in ((w1s, w1), (w2s, w2), (w3s, w3)):
                    sp.dma_start(dst[:, :, :], src.rearrange("(k p) n -> p k n", p=P)).then_inc(loaded, 16)
                with sp.Fori(0, CH) as c:
                    hold(sp, sp_passed, x1_done, c + 1)
                    sp.dma_start(xt[:, :, :],
                                 x[bass.ds(c * CB, CB), :, :].rearrange("b (h p) m -> p (b h) m", p=P)).then_inc(in_loaded, 16)
                    for d in range(DIRS):
                        sp.dma_start(gs[:, d, :, :], scr["g"][bass.ds(c + d * CH, 1), :, :]
                                     .rearrange("a (k p) n -> p (a k) n", p=P)).then_inc(in_loaded, 16)

            @block.tensor
            def _(pe):
                pe.sem_inc(full, 1)
                pe.wait_ge(loaded, 16 * NW)
                pe.wait_ge(made, 3)
                with pe.Fori(0, CH) as c:
                    pe.wait_ge(in_loaded, (c + 1) * 48)
                    pe.wait_ge(copied, c * 2 + 1)
                    for d in range(DIRS):
                        for m in range(MB):
                            n = (OF, OB)[d] + m
                            for k in range(JB):
                                last = nc.tensor.matmul(bank[n][:, :], wo[:, d, k, m * P:(m + 1) * P], gs[:, d, k, :],
                                                        start=(k == 0), stop=(k == JB - 1))
                            last.then_inc(full, 1)
                    for m in range(MB):
                        for t in range(TB):
                            last = nc.tensor.transpose(bank[XT + m][:, t * P:(t + 1) * P],
                                                       xt[:, t, m * P:(m + 1) * P], ident[:])
                        last.then_inc(full, 1)
                    pe.wait_ge(x1_done, c + 2)
                    for m in range(MB):
                        last = nc.tensor.matmul(bank[MEAN][:, :], mean_w[:], x1[:, m, :], start=(m == 0), stop=(m == MB - 1))
                    last.then_inc(full, 1)
                    pe.wait_ge(sq_done, c + 1)
                    for m in range(MB):
                        last = nc.tensor.matmul(bank[VAR][:, :], mean_w[:], sq[:, m, :], start=(m == 0), stop=(m == MB - 1))
                    last.then_inc(full, 1)
                    pe.wait_ge(h2_done, c + 1)
                    for j in range(JB):
                        for e, w in enumerate((w1s, w2s)):
                            for k in range(MB):
                                last = nc.tensor.matmul(bank[(UP + 2 * j + e) % 8][:, :], w[:, k, j * P:(j + 1) * P],
                                                        h2[:, k, :], start=(k == 0), stop=(k == MB - 1))
                            last.then_inc(full, 1)
                    pe.wait_ge(gate_done, (c + 1) * JB)
                    for m in range(MB):
                        for k in range(JB):
                            last = nc.tensor.matmul(bank[(DOWN + m) % 8][:, :], w3s[:, k, m * P:(m + 1) * P], gate[:, k, :],
                                                    start=(k == 0), stop=(k == JB - 1))
                        last.then_inc(full, 1)
                    pe.wait_ge(x2_done, c + 1)
                    for t in range(TB):
                        for m in range(MB):
                            last = nc.tensor.transpose(bank[(OUT + t // 2) % 8][:, (t % 2 * MB + m) * P:(t % 2 * MB + m + 1) * P],
                                                       x2[:, m, t * P:(t + 1) * P], ident[:])
                        if t % 2:
                            last.then_inc(full, 1)

            @block.scalar
            def _(act):
                act.sem_inc(copied, 1)
                act.sem_inc(stored, 16)
                with act.Fori(0, CH) as c:
                    for m in range(MB):
                        act.wait_ge(full, job_full(c, OF + m))
                        last = nc.scalar.activation(of[:, m, :], bank[OF + m][:, :], ACT.Copy)
                    last.then_inc(of_done, 1)
                    act.wait_ge(xc_done, c + 1)
                    last = nc.scalar.activation(sq[:, :, :], xc[:, :, :], ACT.Square)
                    last.then_inc(sq_done, 1)
                    act.wait_ge(rv_done, c + 1)
                    nc.scalar.activation(rs[:, :], rv[:, :], ACT.Sqrt).then_inc(rs_done, 1)
                    for j in range(JB):
                        act.wait_ge(full, job_full(c, UP + 2 * j))
                        nc.scalar.activation(gate[:, j, :], bank[(UP + 2 * j) % 8][:, :], ACT.Silu).then_inc(silu_done, 1)
                    act.wait_ge(stored, (c + 1) * 16)
                    for e in range(2):
                        act.wait_ge(full, job_full(c, OUT + e))
                        nc.scalar.activation(ot[:, 2 * e:2 * e + 2, :],
                                             bank[(OUT + e) % 8][:, :].rearrange("p (t m) -> p t m", t=2),
                                             ACT.Copy).then_inc(copied, 1)
                    act.wait_ge(copied, c * 2 + 3)
                    act.dma_start(out[bass.ds(c * CB, CB), :, :].rearrange("b (h p) m -> p (b h) m", p=P),
                                  ot[:, :, :]).then_inc(stored, 16)
                act.wait_ge(stored, (CH + 1) * 16)

            @block.vector
            def _(dve):
                dve.sem_inc(x1_done, 1)
                LINKS = 3
                with dve.Fori(0, CH) as c:
                    chain = [0]

                    def link(ins):
                        chain[0] += 1
                        ins.then_inc(order, 1)
                        dve.wait_ge(order, c * LINKS + chain[0])

                    def per_batch(ap, b):
                        return ap[:, b * SEQ:(b + 1) * SEQ]

                    dve.wait_ge(of_done, c + 1)
                    dve.wait_ge(full, job_full(c, OB + MB - 1))
                    nc.vector.tensor_copy(modc[:, :, :], mod[:, :, bass.ds(c * CB, CB)])
                    for m in range(MB):
                        for b in range(CB):
                            last = nc.vector.tensor_tensor(per_batch(of[:, m, :], b), per_batch(of[:, m, :], b),
                                                           per_batch(bank[OB + m][:, :], b)[:, ::-1], ALU.add)
                    link(last)
                    dve.wait_ge(full, job_full(c, XT + MB - 1))
                    for m in range(MB):
                        for b in range(CB):
                            last = nc.vector.scalar_tensor_tensor(
                                out=per_batch(x1[:, m, :], b), in0=per_batch(of[:, m, :], b),
                                scalar=modc[:, GATE1 + m, b:b + 1], in1=per_batch(bank[XT + m][:, :], b),
                                op0=ALU.mult, op1=ALU.add)
                    last.then_inc(x1_done, 1)
                    dve.wait_ge(full, job_full(c, MEAN))
                    for m in range(MB):
                        last = nc.vector.tensor_tensor(xc[:, m, :], x1[:, m, :], bank[MEAN][:, :], ALU.subtract)
                    last.then_inc(xc_done, 1)
                    dve.wait_ge(full, job_full(c, VAR))
                    link(nc.vector.tensor_scalar(ve[:, :], bank[VAR][:, :], EPS, None, ALU.add))
                    nc.vector.reciprocal(rv[:, :], ve[:, :]).then_inc(rv_done, 1)
                    dve.wait_ge(rs_done, c + 1)
                    for m in range(MB):
                        last = nc.vector.tensor_tensor(xm[:, m, :], xc[:, m, :], rs[:, :], ALU.mult)
                    link(last)
                    for m in range(MB):
                        for b in range(CB):
                            last = nc.vector.tensor_scalar(per_batch(h2[:, m, :], b), per_batch(xm[:, m, :], b),
                                                           modc[:, SCALE2 + m, b:b + 1], modc[:, SHIFT2 + m, b:b + 1],
                                                           ALU.mult, ALU.add)
                    last.then_inc(h2_done, 1)
                    for j in range(JB):
                        dve.wait_ge(silu_done, c * JB + (j + 1))
                        dve.wait_ge(full, job_full(c, UP + 2 * j + 1))
                        nc.vector.tensor_tensor(gate[:, j, :], gate[:, j, :], bank[(UP + 2 * j + 1) % 8][:, :],
                                                ALU.mult).then_inc(gate_done, 1)
                    dve.wait_ge(full, job_full(c, DOWN + MB - 1))
                    for m in range(MB):
                        for b in range(CB):
                            last = nc.vector.scalar_tensor_tensor(
                                out=per_batch(x2[:, m, :], b), in0=per_batch(bank[(DOWN + m) % 8][:, :], b),
                                scalar=modc[:, GATE2 + m, b:b + 1], in1=per_batch(x1[:, m, :], b),
                                op0=ALU.mult, op1=ALU.add)
                    last.then_inc(x2_done, 1)
                    assert chain[0] == LINKS


def build(nc, a, out):
    scr = {k: nc.dram_tensor("scratch_" + k, [PASSES, DI, T], fp32).ap() for k in ("xs", "sz", "dt", "g")}
    scr["ut"] = nc.dram_tensor("scratch_ut", [PASSES, T, DI], fp32).ap()
    scr["b"] = nc.dram_tensor("scratch_b", [PASSES, T, DS], fp32).ap()
    scr["c"] = nc.dram_tensor("scratch_c", [PASSES, DS, T], fp32).ap()
    both = lambda name: [a[f"L0_cond_{d}_{name}"] for d in ("fwd", "bwd")]
    with nc.sbuf_tensor("mod", [P, NMOD, BATCH], fp32) as mod:
        project_phase(nc, a["x"], a["cond_1024"], [a["L0_cond_adaln_mamba_w"], a["L0_cond_adaln_mlp_w"]],
                      [a["L0_cond_adaln_mamba_b"], a["L0_cond_adaln_mlp_b"]], both("in_w"), both("xproj_w"),
                      both("dt_bias"), mod, scr)
        scan_phase(nc, both("A_log"), both("D"), scr)
        output_phase(nc, a["x"], both("out_w"), a["L0_cond_mlp_w1"], a["L0_cond_mlp_w2"], a["L0_cond_mlp_w3"],
                     mod, scr, out)


def kernel(**inputs):
    import numpy as _np
    import concourse.bacc as _bacc
    from concourse import mybir as _mybir
    from concourse.bass_utils import run_bass_kernel_spmd as _run

    nc = _bacc.Bacc("TRN2", target_bir_lowering=False, num_devices=1)
    arrays, args = {}, {}
    for name, value in inputs.items():
        v = _np.ascontiguousarray(value)
        arrays[f"in_{name}"] = v
        args[name] = nc.dram_tensor(f"in_{name}", v.shape, _mybir.dt.from_np(v.dtype), kind="ExternalInput").ap()
    out = nc.dram_tensor("out", (BATCH, SEQ, DM), fp32, kind="ExternalOutput").ap()
    build(nc, args, out)
    r = _run(nc, [arrays], core_ids=[0])
    return r.results[0]["out"]
```

```python
import concourse.bass as bass
from concourse import mybir
from contextlib import ExitStack

fp32 = mybir.dt.float32
bf16 = mybir.dt.bfloat16
ALU = mybir.AluOpType
ACT = mybir.ActivationFunctionType

BATCH, SEQ, DM = 16, 256, 256
COND = 256
DI, DS = 512, 64
MLP = 512
EPS = 1e-5
P = 128
CB = 2
CH = BATCH // CB
T = CB * SEQ
TB = T // P
MB = DM // P
CK = COND // P
JB = DI // P
DIRS = 2
PASSES = DIRS * CH
QS, GD = 4, 32
NQ, NG = DS // QS, DI // GD
GJ = P // GD
PW = DI + 2 * DS
SHIFT1, SCALE1, GATE1, SHIFT2, SCALE2, GATE2 = (MB * k for k in range(6))
NMOD = 6 * MB


def hold(sp, count, sem, value):
    sp.wait_ge(sem, value)
    sp.sem_inc(count, 1)


def identity_matrix(pool, tile, made, n):
    pool.memset(tile, 1.0).then_inc(made, 1)
    pool.wait_ge(made, n + 1)
    pool.affine_select(out=tile, in_=tile, compare_op=ALU.is_equal, fill=0.0, base=0,
                       pattern=[[-1, P]], channel_multiplier=1).then_inc(made, 1)


def project_phase(nc, x, cond, w_mod, b_mod, w_in, w_xp, dt_bias, mod, scr):
    ctx = ExitStack()
    with ctx:
        def sb(name, shape, dt=fp32):
            return ctx.enter_context(nc.sbuf_tensor(name, shape, dt))

        def sem(name):
            return ctx.enter_context(nc.semaphore(name))

        ident = sb("a_ident", [P, P])
        win = sb("a_win", [P, DIRS, MB, 2 * DI])
        wxp = sb("a_wxp", [P, DIRS, JB, PW])
        dtb = sb("a_dtb", [P, DIRS, JB])
        wmod = sb("a_wmod", [P, 2, CK, 3 * DM])
        bmod = sb("a_bmod", [P, NMOD])
        condT = sb("a_condT", [P, CK, BATCH])
        modc = sb("a_modc", [P, NMOD, CB])
        xt = sb("a_xt", [P, TB, DM])
        stats = sb("a_stats", [P, TB, 6])
        mv = sb("a_mv", [P, TB, 2])
        rvar = sb("a_rvar", [P, TB])
        rstd = sb("a_rstd", [P, TB])
        veps = sb("a_veps", [P, TB])
        xn = sb("a_xn", [P, TB, DM])
        hT = sb("a_hT", [P, DIRS, MB, T])
        xs = sb("a_xs", [P, DIRS, JB, T])
        sz = sb("a_sz", [P, JB, T])
        pre = sb("a_pre", [P, JB, T])
        ey = sb("a_ey", [P, JB, T])
        ln = sb("a_ln", [P, JB, T])
        wy = sb("a_wy", [P, JB, T])
        nd = sb("a_nd", [P, JB, T])
        dt = sb("a_dt", [P, JB, T])
        u = sb("a_u", [P, JB, T])
        bt = sb("a_bt", [P, TB, DS])
        ct = sb("a_ct", [DS, T])
        uT = sb("a_uT", [P, TB, DI])
        bank = [ctx.enter_context(nc.psum_tensor(f"a_bank{n}", [P, T], fp32)) for n in range(8)]

        sp_passed = sem("a_sp_passed")
        made = sem("a_made")
        loaded = sem("a_loaded")
        w_loaded = sem("a_w_loaded")
        mod_ps = sem("a_mod_ps")
        mod_done = sem("a_mod_done")
        x_loaded = sem("a_x_loaded")
        order = sem("a_order")
        rvar_done = sem("a_rvar_done")
        rstd_done = sem("a_rstd_done")
        xn_done = sem("a_xn_done")
        hT_done = sem("a_hT_done")
        full = sem("a_full")
        evac = sem("a_evac")
        expln = sem("a_expln")
        dt_done = sem("a_dt_done")
        u_done = sem("a_u_done")
        st = {k: sem("a_stored_" + k) for k in ("xs", "sz", "dt", "bc", "ut")}

        XT, XS0, Z0, UT1, DT0, B0, C0 = 0, 2, 6, 10, 14, 18, 19
        XS1, Z1, UT0, DT1, B1, C1, JOBS = 20, 24, 28, 32, 36, 37, 38
        XS, Z, DT, BJ, CJ, UT = (XS0, XS1), (Z0, Z1), (DT0, DT1), (B0, B1), (C0, C1), (UT0, UT1)
        EV = JOBS - 2
        MISSING = TB

        def early(first, n):
            return MISSING if first and n < UT1 else 0

        def job_full(c, n, first=False):
            return c * JOBS + (n + 2 + early(first, n))

        def job_evac(c, n, first=False):
            return c * EV + (n - 1 + EV + early(first, n))

        def chunks(eng, body):
            body(0, True, False)
            with eng.Fori(1, CH - 1) as c:
                body(c, False, False)
            body(CH - 1, False, True)

        with nc.Block() as block:
            @block.gpsimd
            def _(pool):
                identity_matrix(pool, ident[:], made, 0)

            @block.sync
            def _(sp):
                def load_x(c):
                    sp.dma_start(xt[:, :, :],
                                 x[bass.ds(c * CB, CB), :, :].rearrange("b (h p) m -> p (b h) m", p=P)).then_inc(x_loaded, 16)

                load_x(0)
                for k in range(CK):
                    sp.dma_start(condT[:, k, :], cond[:, k * P:(k + 1) * P].rearrange("b p -> p b"),
                                 allow_slow_non_contiguous=True).then_inc(loaded, 16)
                for m in range(2):
                    sp.dma_start(wmod[:, m, :, :], w_mod[m].rearrange("(k p) n -> p k n", p=P)).then_inc(loaded, 16)
                    sp.dma_start(bmod[:, m * 3 * MB:(m + 1) * 3 * MB],
                                 b_mod[m].rearrange("(k p) -> p k", p=P), allow_slow_non_contiguous=True).then_inc(loaded, 16)
                for d in range(DIRS):
                    sp.dma_start(win[:, d, :, :], w_in[d].rearrange("(k p) n -> p k n", p=P)).then_inc(w_loaded, 16)
                    sp.dma_start(wxp[:, d, :, :], w_xp[d].rearrange("(k p) n -> p k n", p=P)).then_inc(w_loaded, 16)
                    sp.dma_start(dtb[:, d, :], dt_bias[d].rearrange("(k p) -> p k", p=P),
                                 allow_slow_non_contiguous=True).then_inc(w_loaded, 16)
                for k in st:
                    sp.sem_inc(st[k], 16)

                def put(dst, src, what):
                    sp.dma_start(dst, src).then_inc(st[what], 16)

                def rows(scratch, c, d):
                    return scratch[bass.ds(c + d * CH, 1), :, :].rearrange("a (k p) n -> p (a k) n", p=P)

                def put_x(c, d, first):
                    hold(sp, sp_passed, evac, job_evac(c, XS[d] + JB - 1, first))
                    put(rows(scr["xs"], c, d), xs[:, d, :, :], "xs")
                    hold(sp, sp_passed, evac, job_evac(c, Z[d] + JB - 1, first))
                    put(rows(scr["sz"], c, d), sz[:, :, :], "sz")

                def put_dt(c, d):
                    hold(sp, sp_passed, evac, job_evac(c, CJ[d]))
                    put(rows(scr["b"], c, d), bt[:, :, :], "bc")
                    put(scr["c"][bass.ds(c + d * CH, 1), :, :].rearrange("a s t -> s (a t)"), ct[:, :], "bc")
                    hold(sp, sp_passed, dt_done, c * DIRS + (d + 1))
                    put(rows(scr["dt"], c, d), dt[:, :, :], "dt")

                def put_ut(c, d, job):
                    hold(sp, sp_passed, evac, job)
                    put(rows(scr["ut"], c, d), uT[:, :, :], "ut")

                def body(c, first, last):
                    if not last:
                        hold(sp, sp_passed, xn_done, c + 2)
                        load_x(c + 1)
                    put_x(c, 0, first)
                    if not first:
                        put_ut(c - 1, 1, job_evac(c, UT1 + TB - 1))
                    put_dt(c, 0)
                    put_x(c, 1, first)
                    put_ut(c, 0, job_evac(c, UT0 + TB - 1))
                    put_dt(c, 1)

                chunks(sp, body)
                put_ut(CH - 1, 1, job_evac(CH - 1, JOBS + TB - 1))
                for k in ("xs", "sz", "dt", "ut"):
                    sp.wait_ge(st[k], 16 * (PASSES + 1))
                sp.wait_ge(st["bc"], 16 * (2 * PASSES + 1))

            @block.tensor
            def _(pe):
                pe.sem_inc(full, 1 + MISSING)
                pe.wait_ge(loaded, 16 * (CK + 4))
                for m in range(2):
                    for n in range(3 * MB):
                        col = (m * 3 * MB + n) * BATCH
                        for k in range(CK):
                            last = nc.tensor.matmul(bank[7][:, col:col + BATCH], wmod[:, m, k, n * P:(n + 1) * P],
                                                    condT[:, k, :], start=(k == 0), stop=(k == CK - 1))
                last.then_inc(mod_ps, 1)
                pe.wait_ge(mod_done, 1)
                pe.wait_ge(made, 2)

                def free(c, n, first):
                    if n in (XT + 8, XT + 9):
                        pe.wait_ge(hT_done, c * 8 + 8)
                    elif n >= 8:
                        before = n - 8
                        if first and UT1 <= before < UT1 + MISSING:
                            before -= 8
                        pe.wait_ge(evac, job_evac(c, before, first))
                    elif not first:
                        before = max(k for k in range(JOBS) if k % 8 == n)
                        pe.wait_ge(evac, c * EV + (before - 1))

                def channels(c, job, first, weights, src, kk):
                    for j in range(JB):
                        n = job + j
                        free(c, n, first)
                        for k in range(kk):
                            last = nc.tensor.matmul(bank[n % 8][:, :], weights(k, j), src(k),
                                                    start=(k == 0), stop=(k == kk - 1))
                        last.then_inc(full, 1)

                def xz(c, d, first):
                    pe.wait_ge(hT_done, c * 8 + (6 + 2 * d))
                    channels(c, XS[d], first, lambda k, j: win[:, d, k, j * P:(j + 1) * P], lambda k: hT[:, d, k, :], MB)
                    channels(c, Z[d], first, lambda k, j: win[:, d, k, DI + j * P:DI + (j + 1) * P],
                             lambda k: hT[:, d, k, :], MB)

                def dtbc(c, d, first):
                    pe.wait_ge(evac, job_evac(c, XS[d] + JB - 1, first))
                    channels(c, DT[d], first, lambda k, j: wxp[:, d, k, j * P:(j + 1) * P], lambda k: xs[:, d, k, :], JB)
                    free(c, BJ[d], first)
                    for t in range(TB):
                        for k in range(JB):
                            last = nc.tensor.matmul(bank[BJ[d] % 8][:, t * DS:(t + 1) * DS],
                                                    xs[:, d, k, t * P:(t + 1) * P], wxp[:, d, k, DI:DI + DS],
                                                    start=(k == 0), stop=(k == JB - 1))
                    last.then_inc(full, 1)
                    free(c, CJ[d], first)
                    for k in range(JB):
                        last = nc.tensor.matmul(bank[CJ[d] % 8][0:DS, :], wxp[:, d, k, DI + DS:PW],
                                                xs[:, d, k, :], start=(k == 0), stop=(k == JB - 1))
                    last.then_inc(full, 1)

                def turn_u(c, job, n_u):
                    pe.wait_ge(u_done, n_u)
                    for t in range(TB):
                        n = job + t
                        free(c, n, False)
                        for j in range(JB):
                            last = nc.tensor.transpose(bank[n % 8][:, j * P:(j + 1) * P],
                                                       u[:, j, t * P:(t + 1) * P], ident[:])
                        last.then_inc(full, 1)

                def body(c, first, last):
                    pe.wait_ge(xn_done, c + 2)
                    for k in range(MB):
                        free(c, XT + k, first)
                        for t in range(TB):
                            turned = nc.tensor.transpose(bank[XT + k][:, t * P:(t + 1) * P],
                                                         xn[:, t, k * P:(k + 1) * P], ident[:])
                        turned.then_inc(full, 1)
                    if first:
                        pe.wait_ge(w_loaded, 16 * 3 * DIRS)
                    xz(c, 0, first)
                    if not first:
                        turn_u(c, UT1, c * DIRS + 1)
                    dtbc(c, 0, first)
                    xz(c, 1, first)
                    turn_u(c, UT0, c * DIRS + 2)
                    dtbc(c, 1, first)

                chunks(pe, body)
                turn_u(CH - 1, JOBS, CH * DIRS + 1)

            @block.scalar
            def _(act):
                act.sem_inc(evac, EV + MISSING)
                act.wait_ge(w_loaded, 16 * 3 * DIRS)

                def root(c):
                    act.wait_ge(rvar_done, c + 1)
                    nc.scalar.activation(rstd[:, :], rvar[:, :], ACT.Sqrt).then_inc(rstd_done, 1)

                def silu_xz(c, d, first):
                    act.wait_ge(st["xs"], (c * DIRS + (d + 1)) * 16)
                    for j in range(JB):
                        act.wait_ge(full, job_full(c, XS[d] + j, first))
                        nc.scalar.activation(xs[:, d, j, :], bank[(XS[d] + j) % 8][:, :], ACT.Silu).then_inc(evac, 1)
                    act.wait_ge(st["sz"], (c * DIRS + (d + 1)) * 16)
                    for j in range(JB):
                        act.wait_ge(full, job_full(c, Z[d] + j, first))
                        nc.scalar.activation(sz[:, j, :], bank[(Z[d] + j) % 8][:, :], ACT.Silu).then_inc(evac, 1)

                def softplus_bc(c, d):
                    act.wait_ge(u_done, c * DIRS + (d + 1))
                    for j in range(JB):
                        src = bank[(DT[d] + j) % 8][:, :]
                        act.wait_ge(full, job_full(c, DT[d] + j))
                        nc.scalar.activation(pre[:, j, :], src, ACT.Identity, bias=dtb[:, d, j:j + 1])
                        nc.scalar.activation(ey[:, j, :], src, ACT.Abs, bias=dtb[:, d, j:j + 1]).then_inc(evac, 1)
                    act.wait_ge(st["bc"], (c * DIRS + d) * 32 + 16)
                    act.wait_ge(full, job_full(c, BJ[d]))
                    nc.scalar.activation(bt[:, :, :], bank[BJ[d] % 8][:, 0:TB * DS].rearrange("p (t s) -> p t s", t=TB),
                                         ACT.Copy).then_inc(evac, 1)
                    act.wait_ge(full, job_full(c, CJ[d]))
                    nc.scalar.activation(ct[:, :], bank[CJ[d] % 8][0:DS, :], ACT.Copy).then_inc(evac, 1)
                    act.wait_ge(evac, job_evac(c, DT[d] + JB - 1))
                    nc.scalar.activation(ey[:, :, :], ey[:, :, :], ACT.Exp, scale=-1.0).then_inc(expln, 1)
                    act.wait_ge(expln, c * 4 + (2 * d + 1))
                    nc.scalar.activation(ln[:, :, :], ey[:, :, :], ACT.Ln, bias=1.0).then_inc(expln, 1)

                def copy_ut(c, job, n_stored):
                    act.wait_ge(st["ut"], n_stored)
                    for t in range(TB):
                        act.wait_ge(full, job_full(c, job + t))
                        nc.scalar.activation(uT[:, t, :], bank[(job + t) % 8][:, :], ACT.Copy).then_inc(evac, 1)

                def body(c, first, last):
                    for k in range(MB):
                        act.wait_ge(full, job_full(c, XT + k, first))
                        for d in range(DIRS):
                            for b in range(CB):
                                src = bank[XT + k][:, b * SEQ:(b + 1) * SEQ]
                                nc.scalar.activation(hT[:, d, k, b * SEQ:(b + 1) * SEQ],
                                                     src if d == 0 else src[:, ::-1], ACT.Identity,
                                                     scale=modc[:, SCALE1 + k, b:b + 1],
                                                     bias=modc[:, SHIFT1 + k, b:b + 1]).then_inc(hT_done, 1)
                    silu_xz(c, 0, first)
                    if not first:
                        copy_ut(c, UT1, c * (DIRS * 16))
                    softplus_bc(c, 0)
                    silu_xz(c, 1, first)
                    if not last:
                        root(c + 1)
                    copy_ut(c, UT0, c * (DIRS * 16) + 16)
                    softplus_bc(c, 1)

                root(0)
                chunks(act, body)
                copy_ut(CH - 1, JOBS, CH * DIRS * 16)

            @block.vector
            def _(dve):
                dve.sem_inc(xn_done, 1)
                dve.sem_inc(u_done, 1)
                LN_LINKS, SP_LINKS = 3, 2

                def link(ins, n):
                    ins.then_inc(order, 1)
                    dve.wait_ge(order, n)

                def norm(c, n):
                    dve.wait_ge(x_loaded, (c + 1) * 16)
                    for t in range(TB):
                        last = nc.vector.bn_stats(stats[:, t, :], xt[:, t, :])
                    link(last, n + 1)
                    start = isinstance(c, int) and c == 0
                    if not start:
                        nc.vector.tensor_copy(modc[:, :, :], mod[:, :, bass.ds(c * CB, CB)])
                    for t in range(TB):
                        last = nc.vector.bn_aggr(mv[:, t, :], stats[:, t, :])
                    link(last, n + 2)
                    link(nc.vector.tensor_scalar(veps[:, :], mv[:, :, 1], EPS, None, ALU.add), n + 3)
                    nc.vector.reciprocal(rvar[:, :], veps[:, :]).then_inc(rvar_done, 1)
                    if start:
                        dve.wait_ge(loaded, 16 * (CK + 4))
                        dve.wait_ge(mod_ps, 1)
                        for k in range(NMOD):
                            one = 1.0 if k in (SCALE1, SCALE1 + 1, SCALE2, SCALE2 + 1) else 0.0
                            last = nc.vector.tensor_scalar(mod[:, k, :], bank[7][:, k * BATCH:(k + 1) * BATCH],
                                                           bmod[:, k:k + 1], one, ALU.add, ALU.add)
                        last.then_inc(mod_done, 1)
                        dve.wait_ge(mod_done, 1)
                        nc.vector.tensor_copy(modc[:, :, :], mod[:, :, 0:CB])
                    dve.wait_ge(rstd_done, c + 1)
                    for t in range(TB):
                        last = nc.vector.tensor_scalar(xn[:, t, :], xt[:, t, :], mv[:, t, 0:1], rstd[:, t:t + 1],
                                                       ALU.subtract, ALU.mult)
                    last.then_inc(xn_done, 1)

                def softplus(c, d, n):
                    dve.wait_ge(expln, c * 4 + (2 * d + 2))
                    link(nc.vector.tensor_scalar(wy[:, :, :], ey[:, :, :], 1.0, None, ALU.add), n + 1)
                    nc.vector.scalar_tensor_tensor(out=nd[:, :, :], in0=wy[:, :, :], scalar=-1.0, in1=ey[:, :, :],
                                                   op0=ALU.add, op1=ALU.subtract)
                    link(nc.vector.scalar_tensor_tensor(out=ln[:, :, :], in0=pre[:, :, :], scalar=0.0, in1=ln[:, :, :],
                                                        op0=ALU.max, op1=ALU.add), n + 2)
                    dve.wait_ge(st["dt"], (c * DIRS + (d + 1)) * 16)
                    nc.vector.tensor_tensor(dt[:, :, :], ln[:, :, :], nd[:, :, :], ALU.subtract).then_inc(dt_done, 1)
                    dve.wait_ge(dt_done, c * DIRS + (d + 1))

                def body(c, first, last):
                    n = c * (LN_LINKS + 2 * SP_LINKS) + LN_LINKS
                    softplus(c, 0, n)
                    if not first:
                        dve.wait_ge(full, job_full(c, UT1 + TB - 1))
                    nc.vector.tensor_tensor(u[:, :, :], dt[:, :, :], xs[:, 0, :, :], ALU.mult).then_inc(u_done, 1)
                    n = n + SP_LINKS
                    if not last:
                        norm(c + 1, n)
                        n = n + LN_LINKS
                    softplus(c, 1, n)
                    dve.wait_ge(full, job_full(c, UT0 + TB - 1))
                    nc.vector.tensor_tensor(u[:, :, :], dt[:, :, :], xs[:, 1, :, :], ALU.mult).then_inc(u_done, 1)

                norm(0, 0)
                chunks(dve, body)


def scan_phase(nc, a_log, d_skip, scr):
    ctx = ExitStack()
    with ctx:
        def sb(name, shape, dt=fp32):
            return ctx.enter_context(nc.sbuf_tensor(name, shape, dt))

        def pb(name):
            return ctx.enter_context(nc.psum_tensor(name, [P, T], fp32))

        def sem(name):
            return ctx.enter_context(nc.semaphore(name))

        NDA = 8
        UPQ = NG
        UPP = NQ * UPQ
        GPQ = UPQ // GJ
        NV = UPQ // 4
        AT_ACT = {g: n for n, g in enumerate((0, 2, 4, 5, 7, 9, 10, 12, 13))}
        AT_DVE = {g: n + len(AT_ACT) for n, g in enumerate((0, 2, 4, 6, 8, 10, 12))}
        NPROD = TB * QS
        assert len(AT_ACT) + len(AT_DVE) == NPROD
        LOAD = QS * 16

        ident = sb("b_ident", [P, P])
        summer = sb("b_summer", [P, GD])
        zero = sb("b_zero", [P, T], bf16)
        negA = sb("b_negA", [P, DIRS, NG, NQ])
        dskip = sb("b_dskip", [P, DIRS, JB])
        dtr = sb("b_dtr", [P, NG, T])
        uT = sb("b_uT", [P, TB, DI])
        bt = sb("b_bt", [P, TB, DS])
        crep = sb("b_crep", [P, 2, T])
        ub = sb("b_ub", [P, 2, TB, NG, QS, GD])
        dA = sb("b_dA", [P, NDA, CB, SEQ])
        hc = sb("b_hc", [P, NG, T])
        xs = sb("b_xs", [P, JB, T])
        sz = sb("b_sz", [P, JB, T])
        y = [pb(f"b_y{j}") for j in range(JB)]
        inp = [pb("b_in0"), pb("b_in1")]
        inv = [pb("b_in2"), pb("b_in3")]

        sp_passed = sem("b_sp_passed")
        made = sem("b_made")
        loaded = sem("b_loaded")
        a_exp = sem("b_a_exp")
        a_done = sem("b_a_done")
        cleared = sem("b_cleared")
        dt_loaded = [sem(f"b_dt_loaded{j}") for j in range(JB)]
        ut_loaded = sem("b_ut_loaded")
        c_loaded = [sem("b_c_loaded0"), sem("b_c_loaded1")]
        xz_loaded = sem("b_xz_loaded")
        prod_act = sem("b_prod_act")
        prod_dve = sem("b_prod_dve")
        exp_done = sem("b_exp_done")
        turned = sem("b_turned")
        scanned = sem("b_scanned")
        hc_pool = sem("b_hc_pool")
        hc_dve = sem("b_hc_dve")
        summed = sem("b_summed")
        y_read = sem("b_y_read")
        gated = sem("b_gated")
        stored = sem("b_stored")

        def is_v(g):
            return g % 4 == 3

        p_units = [g for g in range(UPQ) if not is_v(g)]
        H = NQ // 2

        def passes(eng, one_pass, direction=False):
            if not direction:
                one_pass(0, 0, True, False)
                with eng.Fori(1, PASSES - 1) as p:
                    one_pass(p, None, False, False)
                one_pass(PASSES - 1, None, False, True)
                return
            one_pass(0, 0, True, False)
            with eng.Fori(1, CH) as c:
                one_pass(c, 0, False, False)
            with eng.Fori(0, CH - 1) as c:
                one_pass(c + CH, 1, False, False)
            one_pass(PASSES - 1, 1, False, True)

        def halves(eng, half_pass):
            half_pass(0, True, False)
            with eng.Fori(1, H - 1) as half:
                half_pass(half, False, False)
            half_pass(H - 1, False, True)

        with nc.Block() as block:
            @block.sync
            def _(sp):
                for d in range(DIRS):
                    for i in range(QS):
                        sp.dma_start(negA[i * GD:(i + 1) * GD, d, :, :],
                                     a_log[d][:, i * NQ:(i + 1) * NQ].rearrange("(g d) q -> d g q", d=GD)).then_inc(loaded, 16)
                    sp.dma_start(dskip[:, d, :], d_skip[d].rearrange("(k p) -> p k", p=P),
                                 allow_slow_non_contiguous=True).then_inc(loaded, 16)

                def one(scratch, p):
                    return scratch[bass.ds(p, 1), :, :]

                def rows(scratch, p):
                    return one(scratch, p).rearrange("a (k p) n -> p (a k) n", p=P)

                def load_u(p):
                    sp.dma_start(uT[:, :, :], rows(scr["ut"], p)).then_inc(ut_loaded, 16)
                    sp.dma_start(bt[:, :, :], rows(scr["b"], p)).then_inc(ut_loaded, 16)

                def load_dt(p, j):
                    for i in range(QS):
                        sp.dma_start(dtr[i * GD:(i + 1) * GD, j * GJ:(j + 1) * GJ, :],
                                     one(scr["dt"], p)[:, j * P:(j + 1) * P, :]
                                     .rearrange("a (g d) t -> d (a g) t", d=GD)).then_inc(dt_loaded[j], 16)

                def load_c(p, q, k):
                    for i in range(QS):
                        sp.dma_start(crep[i * GD:(i + 1) * GD, k, :],
                                     one(scr["c"], p)[:, bass.ds(q + (i * NQ + k), 1), :]
                                     .rearrange("a s t -> (a s) t").broadcast_to((GD, T))).then_inc(c_loaded[k], 16)

                def c_used(n):
                    hold(sp, sp_passed, hc_pool, (n + 1) * GPQ + 1)
                    hold(sp, sp_passed, hc_dve, (n + 1) * NV + 2)

                load_u(0)
                load_c(0, 0, 0)
                for j in range(JB):
                    load_dt(0, j)
                load_c(0, 0, 1)

                def one_pass(p, d, first, last):
                    if not first:
                        hold(sp, sp_passed, gated, p * JB + 1)
                        sp.dma_start(rows(scr["g"], p - 1), xs[:, :, :]).then_inc(stored, 16)
                        hold(sp, sp_passed, stored, p * 16)
                    sp.dma_start(xs[:, :, :], rows(scr["xs"], p)).then_inc(xz_loaded, 16)
                    sp.dma_start(sz[:, :, :], rows(scr["sz"], p)).then_inc(xz_loaded, 16)
                    with sp.Fori(1, H) as half:
                        for k in range(2):
                            c_used((p * NQ + half * 2) + (k - 2))
                            load_c(p, half * 2, k)
                    if not last:
                        hold(sp, sp_passed, prod_act, (p + 1) * NQ + 1)
                        hold(sp, sp_passed, prod_dve, (p + 1) * NQ + 1)
                        load_u(p + 1)
                        c_used(p * NQ + (NQ - 2))
                        load_c(p + 1, 0, 0)
                        for j in range(JB):
                            hold(sp, sp_passed, exp_done, p * UPP + (UPP - UPQ + (j + 1) * GJ + 1))
                            load_dt(p + 1, j)
                        c_used(p * NQ + (NQ - 1))
                        load_c(p + 1, 0, 1)

                passes(sp, one_pass)
                sp.wait_ge(gated, PASSES * JB + 1)
                sp.dma_start(scr["g"][PASSES - 1].rearrange("(k p) n -> p k n", p=P), xs[:, :, :]).then_inc(stored, 16)
                sp.wait_ge(stored, 16 * PASSES)

            @block.gpsimd
            def _(pool):
                identity_matrix(pool, ident[:], made, 0)
                pool.memset(summer[:], 0.0).then_inc(made, 1)
                for i in range(QS):
                    pool.wait_ge(made, 3 + i)
                    pool.affine_select(out=summer[:], in_=summer[:], compare_op=ALU.not_equal, fill=1.0, base=-i * GD,
                                       pattern=[[-1, GD]], channel_multiplier=1).then_inc(made, 1)
                pool.memset(zero[:], 0.0).then_inc(made, 1)
                pool.sem_inc(hc_pool, 1)
                pool.sem_inc(gated, 1)

                def gate(p):
                    pool.wait_ge(xz_loaded, (p + 1) * 32)
                    for j in range(JB):
                        pool.wait_ge(y_read, p * JB + (j + 1 + JB))
                        nc.gpsimd.tensor_tensor(xs[:, j, :], xs[:, j, :], sz[:, j, :], ALU.mult).then_inc(gated, 1)

                def quad(p, half, k, gate_before):
                    U = (p * NQ + half * 2) * UPQ
                    pool.wait_ge(c_loaded[k], (p * H + half + 1) * LOAD)
                    for j in range(GPQ):
                        mine = slice(j * GJ, j * GJ + GJ - 1)
                        pool.wait_ge(scanned, U + (k * UPQ + mine.stop + NDA))
                        nc.gpsimd.tensor_tensor(hc[:, mine, :], hc[:, mine, :],
                                                crep[:, k:k + 1, :].broadcast_to((P, GJ - 1, T)), ALU.mult).then_inc(hc_pool, 1)
                        if gate_before and j == GPQ - 1:
                            gate(p - 1)

                def one_pass(p, d, first, last):
                    quad(p, 0, 0, not first)
                    quad(p, 0, 1, False)
                    with pool.Fori(1, H) as half:
                        quad(p, half, 0, False)
                        quad(p, half, 1, False)

                passes(pool, one_pass)
                gate(PASSES - 1)

            @block.scalar
            def _(act):
                act.sem_inc(exp_done, 1)
                act.sem_inc(prod_act, 1)
                act.wait_ge(loaded, 16 * DIRS * (QS + 1))
                nc.scalar.activation(negA[:, :, :, :], negA[:, :, :, :], ACT.Exp).then_inc(a_exp, 1)
                act.wait_ge(a_done, 1)
                act.wait_ge(cleared, 1)

                def product(n, k, col):
                    t, i = divmod(n, QS)
                    return nc.scalar.activation(ub[:, k, t, :, i, :], uT[:, t, :].rearrange("p (g d) -> p g d", g=NG),
                                                ACT.Copy, scale=bt[:, t, bass.ds(col + i * NQ, 1)])

                def quad(p, d, half, k, first, wrap, nxt):
                    U = (p * NQ + half * 2) * UPQ
                    for g in range(UPQ):
                        if first and g % GJ == 0:
                            act.wait_ge(dt_loaded[g // GJ], (p + 1) * LOAD)
                        act.wait_ge(scanned, U + (k * UPQ + g + 1))
                        nc.scalar.activation(dA[:, g % NDA, :, 1:SEQ],
                                             dtr[:, g, :].rearrange("p (b t) -> p b t", b=CB)[:, :, 1:SEQ], ACT.Exp,
                                             scale=negA[:, d, g, bass.ds(half * 2 + k, 1)]).then_inc(exp_done, 1)
                        if nxt and g in AT_ACT:
                            if g == 0:
                                act.wait_ge(turned, U + (k * UPQ + 1))
                                if wrap:
                                    act.wait_ge(ut_loaded, (p + 2) * 32)
                            last = product(AT_ACT[g], (k + 1) % 2, 0 if wrap else half * 2 + (k + 1))
                            if AT_ACT[g] == len(AT_ACT) - 1:
                                last.then_inc(prod_act, 1)

                def one_pass(p, d, first, last):
                    def half_pass(half, h_first, h_last):
                        quad(p, d, half, 0, h_first, False, True)
                        quad(p, d, half, 1, False, h_last, not (h_last and last))

                    halves(act, half_pass)

                act.wait_ge(ut_loaded, 32)
                for n in sorted(AT_ACT.values()):
                    last = product(n, 0, 0)
                last.then_inc(prod_act, 1)
                passes(act, one_pass, direction=True)

            @block.vector
            def _(dve):
                dve.sem_inc(scanned, NDA)
                dve.sem_inc(hc_dve, 2)
                dve.sem_inc(prod_dve, 1)
                dve.sem_inc(y_read, JB)
                nc.vector.memset(dA[:, :, :, :], 0.0).then_inc(cleared, 1)
                dve.wait_ge(a_exp, 1)
                nc.vector.tensor_scalar(negA[:, :, :, :], negA[:, :, :, :], -1.0, None, ALU.mult).then_inc(a_done, 1)
                dve.wait_ge(cleared, 1)

                def product(n, k, col):
                    t, i = divmod(n, QS)
                    return nc.vector.tensor_scalar(ub[:, k, t, :, i, :], uT[:, t, :].rearrange("p (g d) -> p g d", g=NG),
                                                   bt[:, t, bass.ds(col + i * NQ, 1)], None, ALU.mult)

                def times_c(p, half, k, g):
                    U = (p * NQ + half * 2) * UPQ
                    if g == 3:
                        dve.wait_ge(c_loaded[k], (p * H + half + 1) * LOAD)
                    dve.wait_ge(scanned, U + (k * UPQ + g + 1 + NDA))
                    nc.vector.tensor_tensor(hc[:, g, :], inv[g // 4 % 2][:, :], crep[:, k, :], ALU.mult).then_inc(hc_dve, 1)

                def read_y(p, d, j):
                    if j == 0:
                        dve.wait_ge(xz_loaded, (p + 1) * 32)
                    dve.wait_ge(summed, (p + 1) * (NQ * GPQ) - (JB - 1 - j) + GPQ)
                    nc.vector.scalar_tensor_tensor(out=xs[:, j, :], in0=xs[:, j, :], scalar=dskip[:, d, j:j + 1],
                                                   in1=y[j][:, :], op0=ALU.mult, op1=ALU.add).then_inc(y_read, 1)

                def quad(p, half, k, wrap, nxt, read_before):
                    U = (p * NQ + half * 2) * UPQ
                    G = (p * NQ + half * 2) * GPQ
                    for g in range(UPQ):
                        dve.wait_ge(exp_done, U + (k * UPQ + g + 1 + 1))
                        dve.wait_ge(turned, U + (k * UPQ + g + 1 + 1))
                        if g % GJ == 0:
                            dve.wait_ge(summed, G + (k * GPQ + g // GJ + 1))
                        if is_v(g):
                            bank = inv[g // 4 % 2][:, :]
                            out = bank
                        else:
                            bank = inp[p_units.index(g) % 2][:, :]
                            out = hc[:, g, :]
                        nc.vector.tensor_tensor_scan(out, dA[:, g % NDA, :, :].rearrange("p b t -> p (b t)"), bank, 0.0,
                                                     ALU.mult, ALU.add).then_inc(scanned, 1)
                        if g and is_v(g - 1):
                            times_c(p, half, k, g - 1)
                        if nxt and g in AT_DVE:
                            if g == 0:
                                dve.wait_ge(turned, U + (k * UPQ + 1))
                                if wrap:
                                    dve.wait_ge(ut_loaded, (p + 2) * 32)
                            last = product(AT_DVE[g], (k + 1) % 2, 0 if wrap else half * 2 + (k + 1))
                            if AT_DVE[g] == NPROD - 1:
                                last.then_inc(prod_dve, 1)
                        if read_before is not None and 8 <= g < 8 + JB:
                            read_y(p - 1, read_before, g - 8)
                    times_c(p, half, k, UPQ - 1)

                def one_pass(p, d, first, last, d_before):
                    def half_pass(half, h_first, h_last):
                        quad(p, half, 0, False, True, d_before if h_first else None)
                        quad(p, half, 1, h_last, not (h_last and last), None)

                    halves(dve, half_pass)

                dve.wait_ge(ut_loaded, 32)
                for n in sorted(AT_DVE.values()):
                    last = product(n, 0, 0)
                last.then_inc(prod_dve, 1)
                one_pass(0, 0, True, False, None)
                with dve.Fori(1, CH + 1) as p:
                    one_pass(p, None, False, False, 0)
                with dve.Fori(CH + 1, PASSES - 1) as p:
                    one_pass(p, None, False, False, 1)
                one_pass(PASSES - 1, None, False, True, 1)
                for j in range(JB):
                    read_y(PASSES - 1, 1, j)

            @block.tensor
            def _(pe):
                pe.sem_inc(turned, 1)
                pe.sem_inc(summed, GPQ)
                pe.wait_ge(made, 3 + QS + 1)

                def turn(p, half, k, j):
                    Q = p * NQ + half * 2
                    kk, jj = (k + j // GPQ) % 2, j % GPQ
                    if jj == 0:
                        pe.wait_ge(prod_act, Q + (k + j // GPQ + 1 + 1))
                        pe.wait_ge(prod_dve, Q + (k + j // GPQ + 1 + 1))
                    for e in range(GJ):
                        g = jj * GJ + e
                        if is_v(g):
                            pe.wait_ge(hc_dve, Q * NV + (k * NV + j + 1))
                            bank = inv[g // 4 % 2]
                        else:
                            n = p_units.index(g)
                            user = p_units[n - 2] - (UPQ if n < 2 else 0)
                            pe.wait_ge(scanned, Q * UPQ + (k * UPQ + (j - jj) * GJ + user + 1 + NDA))
                            bank = inp[n % 2]
                        for t in range(TB):
                            last = nc.tensor.transpose(bank[:, t * P:(t + 1) * P],
                                                       ub[:, kk, t, g, :, :].rearrange("p i d -> p (i d)"), ident[:])
                        last.then_inc(turned, 1)

                def add(p, half, k, j, start, stop):
                    Q = p * NQ + half * 2
                    if start:
                        pe.wait_ge(y_read, p * JB + (j + 1))
                        nc.tensor.matmul(y[j][:, :], zero[:, 0:P], zero[:, :], start=True, stop=False,
                                         skip_group_check=True)
                    pe.wait_ge(hc_pool, Q * GPQ + (k * GPQ + j + 1 + 1))
                    pe.wait_ge(hc_dve, Q * NV + (k * NV + j + 1 + 2))
                    for e in range(GJ):
                        last = nc.tensor.matmul(y[j][e * GD:(e + 1) * GD, :], summer[:, :], hc[:, j * GJ + e, :],
                                                start=False, stop=stop, tile_position=(0, e * GD), skip_group_check=True)
                    last.then_inc(summed, 1)

                def one_pass(p, d, first, last):
                    def half_pass(half, h_first, h_last):
                        for k in range(2):
                            for j in range(GPQ):
                                if not (h_last and last and k == 1 and j >= 2):
                                    turn(p, half, k, j + 2)
                                add(p, half, k, j, h_first and k == 0, h_last and k == 1)

                    halves(pe, half_pass)

                turn(0, 0, 0, 0)
                turn(0, 0, 0, 1)
                passes(pe, one_pass)


def output_phase(nc, x, w_out, w1, w2, w3, mod, scr, out):
    ctx = ExitStack()
    with ctx:
        def sb(name, shape, dt=fp32):
            return ctx.enter_context(nc.sbuf_tensor(name, shape, dt))

        def sem(name):
            return ctx.enter_context(nc.semaphore(name))

        ident = sb("c_ident", [P, P])
        mean_w = sb("c_mean_w", [P, P])
        wo = sb("c_wo", [P, DIRS, JB, DM])
        w1s = sb("c_w1", [P, MB, MLP])
        w2s = sb("c_w2", [P, MB, MLP])
        w3s = sb("c_w3", [P, JB, DM])
        modc = sb("c_modc", [P, NMOD, CB])
        xt = sb("c_xt", [P, TB, DM])
        gs = sb("c_gs", [P, DIRS, JB, T])
        of = sb("c_of", [P, MB, T])
        x1 = sb("c_x1", [P, MB, T])
        xc = sb("c_xc", [P, MB, T])
        sq = sb("c_sq", [P, MB, T])
        ve = sb("c_ve", [P, T])
        rv = sb("c_rv", [P, T])
        rs = sb("c_rs", [P, T])
        xm = sb("c_xm", [P, MB, T])
        h2 = sb("c_h2", [P, MB, T])
        gate = sb("c_gate", [P, JB, T])
        x2 = sb("c_x2", [P, MB, T])
        ot = sb("c_ot", [P, TB, DM])
        bank = [ctx.enter_context(nc.psum_tensor(f"c_bank{n}", [P, T], fp32)) for n in range(8)]
        OF, OB, XT, MEAN, VAR, UP, DOWN, OUT, JOBS = 0, 2, 4, 6, 7, 8, 16, 18, 20

        sp_passed = sem("c_sp_passed")
        made = sem("c_made")
        loaded = sem("c_loaded")
        in_loaded = sem("c_in_loaded")
        full = sem("c_full")
        of_done = sem("c_of_done")
        order = sem("c_order")
        x1_done = sem("c_x1_done")
        xc_done = sem("c_xc_done")
        sq_done = sem("c_sq_done")
        rv_done = sem("c_rv_done")
        rs_done = sem("c_rs_done")
        h2_done = sem("c_h2_done")
        silu_done = sem("c_silu_done")
        gate_done = sem("c_gate_done")
        x2_done = sem("c_x2_done")
        copied = sem("c_copied")
        stored = sem("c_stored")

        def job_full(c, n):
            return c * JOBS + (n + 2)

        NW = DIRS + 3
        with nc.Block() as block:
            @block.gpsimd
            def _(pool):
                identity_matrix(pool, ident[:], made, 0)
                pool.memset(mean_w[:], 1.0 / DM).then_inc(made, 1)

            @block.sync
            def _(sp):
                for d in range(DIRS):
                    sp.dma_start(wo[:, d, :, :], w_out[d].rearrange("(k p) n -> p k n", p=P)).then_inc(loaded, 16)
                for dst, src in ((w1s, w1), (w2s, w2), (w3s, w3)):
                    sp.dma_start(dst[:, :, :], src.rearrange("(k p) n -> p k n", p=P)).then_inc(loaded, 16)
                with sp.Fori(0, CH) as c:
                    hold(sp, sp_passed, x1_done, c + 1)
                    sp.dma_start(xt[:, :, :],
                                 x[bass.ds(c * CB, CB), :, :].rearrange("b (h p) m -> p (b h) m", p=P)).then_inc(in_loaded, 16)
                    for d in range(DIRS):
                        sp.dma_start(gs[:, d, :, :], scr["g"][bass.ds(c + d * CH, 1), :, :]
                                     .rearrange("a (k p) n -> p (a k) n", p=P)).then_inc(in_loaded, 16)

            @block.tensor
            def _(pe):
                pe.sem_inc(full, 1)
                pe.wait_ge(loaded, 16 * NW)
                pe.wait_ge(made, 3)
                with pe.Fori(0, CH) as c:
                    pe.wait_ge(in_loaded, (c + 1) * 48)
                    pe.wait_ge(copied, c * 2 + 1)
                    for d in range(DIRS):
                        for m in range(MB):
                            n = (OF, OB)[d] + m
                            for k in range(JB):
                                last = nc.tensor.matmul(bank[n][:, :], wo[:, d, k, m * P:(m + 1) * P], gs[:, d, k, :],
                                                        start=(k == 0), stop=(k == JB - 1))
                            last.then_inc(full, 1)
                    for m in range(MB):
                        for t in range(TB):
                            last = nc.tensor.transpose(bank[XT + m][:, t * P:(t + 1) * P],
                                                       xt[:, t, m * P:(m + 1) * P], ident[:])
                        last.then_inc(full, 1)
                    pe.wait_ge(x1_done, c + 2)
                    for m in range(MB):
                        last = nc.tensor.matmul(bank[MEAN][:, :], mean_w[:], x1[:, m, :], start=(m == 0), stop=(m == MB - 1))
                    last.then_inc(full, 1)
                    pe.wait_ge(sq_done, c + 1)
                    for m in range(MB):
                        last = nc.tensor.matmul(bank[VAR][:, :], mean_w[:], sq[:, m, :], start=(m == 0), stop=(m == MB - 1))
                    last.then_inc(full, 1)
                    pe.wait_ge(h2_done, c + 1)
                    for j in range(JB):
                        for e, w in enumerate((w1s, w2s)):
                            for k in range(MB):
                                last = nc.tensor.matmul(bank[(UP + 2 * j + e) % 8][:, :], w[:, k, j * P:(j + 1) * P],
                                                        h2[:, k, :], start=(k == 0), stop=(k == MB - 1))
                            last.then_inc(full, 1)
                    pe.wait_ge(gate_done, (c + 1) * JB)
                    for m in range(MB):
                        for k in range(JB):
                            last = nc.tensor.matmul(bank[(DOWN + m) % 8][:, :], w3s[:, k, m * P:(m + 1) * P], gate[:, k, :],
                                                    start=(k == 0), stop=(k == JB - 1))
                        last.then_inc(full, 1)
                    pe.wait_ge(x2_done, c + 1)
                    for t in range(TB):
                        for m in range(MB):
                            last = nc.tensor.transpose(bank[(OUT + t // 2) % 8][:, (t % 2 * MB + m) * P:(t % 2 * MB + m + 1) * P],
                                                       x2[:, m, t * P:(t + 1) * P], ident[:])
                        if t % 2:
                            last.then_inc(full, 1)

            @block.scalar
            def _(act):
                act.sem_inc(copied, 1)
                act.sem_inc(stored, 16)
                with act.Fori(0, CH) as c:
                    for m in range(MB):
                        act.wait_ge(full, job_full(c, OF + m))
                        last = nc.scalar.activation(of[:, m, :], bank[OF + m][:, :], ACT.Copy)
                    last.then_inc(of_done, 1)
                    act.wait_ge(xc_done, c + 1)
                    last = nc.scalar.activation(sq[:, :, :], xc[:, :, :], ACT.Square)
                    last.then_inc(sq_done, 1)
                    act.wait_ge(rv_done, c + 1)
                    nc.scalar.activation(rs[:, :], rv[:, :], ACT.Sqrt).then_inc(rs_done, 1)
                    for j in range(JB):
                        act.wait_ge(full, job_full(c, UP + 2 * j))
                        nc.scalar.activation(gate[:, j, :], bank[(UP + 2 * j) % 8][:, :], ACT.Silu).then_inc(silu_done, 1)
                    act.wait_ge(stored, (c + 1) * 16)
                    for e in range(2):
                        act.wait_ge(full, job_full(c, OUT + e))
                        nc.scalar.activation(ot[:, 2 * e:2 * e + 2, :],
                                             bank[(OUT + e) % 8][:, :].rearrange("p (t m) -> p t m", t=2),
                                             ACT.Copy).then_inc(copied, 1)
                    act.wait_ge(copied, c * 2 + 3)
                    act.dma_start(out[bass.ds(c * CB, CB), :, :].rearrange("b (h p) m -> p (b h) m", p=P),
                                  ot[:, :, :]).then_inc(stored, 16)
                act.wait_ge(stored, (CH + 1) * 16)

            @block.vector
            def _(dve):
                dve.sem_inc(x1_done, 1)
                LINKS = 3
                with dve.Fori(0, CH) as c:
                    chain = [0]

                    def link(ins):
                        chain[0] += 1
                        ins.then_inc(order, 1)
                        dve.wait_ge(order, c * LINKS + chain[0])

                    def per_batch(ap, b):
                        return ap[:, b * SEQ:(b + 1) * SEQ]

                    dve.wait_ge(of_done, c + 1)
                    dve.wait_ge(full, job_full(c, OB + MB - 1))
                    nc.vector.tensor_copy(modc[:, :, :], mod[:, :, bass.ds(c * CB, CB)])
                    for m in range(MB):
                        for b in range(CB):
                            last = nc.vector.tensor_tensor(per_batch(of[:, m, :], b), per_batch(of[:, m, :], b),
                                                           per_batch(bank[OB + m][:, :], b)[:, ::-1], ALU.add)
                    link(last)
                    dve.wait_ge(full, job_full(c, XT + MB - 1))
                    for m in range(MB):
                        for b in range(CB):
                            last = nc.vector.scalar_tensor_tensor(
                                out=per_batch(x1[:, m, :], b), in0=per_batch(of[:, m, :], b),
                                scalar=modc[:, GATE1 + m, b:b + 1], in1=per_batch(bank[XT + m][:, :], b),
                                op0=ALU.mult, op1=ALU.add)
                    last.then_inc(x1_done, 1)
                    dve.wait_ge(full, job_full(c, MEAN))
                    for m in range(MB):
                        last = nc.vector.tensor_tensor(xc[:, m, :], x1[:, m, :], bank[MEAN][:, :], ALU.subtract)
                    last.then_inc(xc_done, 1)
                    dve.wait_ge(full, job_full(c, VAR))
                    link(nc.vector.tensor_scalar(ve[:, :], bank[VAR][:, :], EPS, None, ALU.add))
                    nc.vector.reciprocal(rv[:, :], ve[:, :]).then_inc(rv_done, 1)
                    dve.wait_ge(rs_done, c + 1)
                    for m in range(MB):
                        last = nc.vector.tensor_tensor(xm[:, m, :], xc[:, m, :], rs[:, :], ALU.mult)
                    link(last)
                    for m in range(MB):
                        for b in range(CB):
                            last = nc.vector.tensor_scalar(per_batch(h2[:, m, :], b), per_batch(xm[:, m, :], b),
                                                           modc[:, SCALE2 + m, b:b + 1], modc[:, SHIFT2 + m, b:b + 1],
                                                           ALU.mult, ALU.add)
                    last.then_inc(h2_done, 1)
                    for j in range(JB):
                        dve.wait_ge(silu_done, c * JB + (j + 1))
                        dve.wait_ge(full, job_full(c, UP + 2 * j + 1))
                        nc.vector.tensor_tensor(gate[:, j, :], gate[:, j, :], bank[(UP + 2 * j + 1) % 8][:, :],
                                                ALU.mult).then_inc(gate_done, 1)
                    dve.wait_ge(full, job_full(c, DOWN + MB - 1))
                    for m in range(MB):
                        for b in range(CB):
                            last = nc.vector.scalar_tensor_tensor(
                                out=per_batch(x2[:, m, :], b), in0=per_batch(bank[(DOWN + m) % 8][:, :], b),
                                scalar=modc[:, GATE2 + m, b:b + 1], in1=per_batch(x1[:, m, :], b),
                                op0=ALU.mult, op1=ALU.add)
                    last.then_inc(x2_done, 1)
                    assert chain[0] == LINKS


def build(nc, a, out):
    scr = {k: nc.dram_tensor("scratch_" + k, [PASSES, DI, T], fp32).ap() for k in ("xs", "sz", "dt", "g")}
    scr["ut"] = nc.dram_tensor("scratch_ut", [PASSES, T, DI], fp32).ap()
    scr["b"] = nc.dram_tensor("scratch_b", [PASSES, T, DS], fp32).ap()
    scr["c"] = nc.dram_tensor("scratch_c", [PASSES, DS, T], fp32).ap()
    both = lambda name: [a[f"L0_cond_{d}_{name}"] for d in ("fwd", "bwd")]
    with nc.sbuf_tensor("mod", [P, NMOD, BATCH], fp32) as mod:
        project_phase(nc, a["x"], a["cond_1024"], [a["L0_cond_adaln_mamba_w"], a["L0_cond_adaln_mlp_w"]],
                      [a["L0_cond_adaln_mamba_b"], a["L0_cond_adaln_mlp_b"]], both("in_w"), both("xproj_w"),
                      both("dt_bias"), mod, scr)
        scan_phase(nc, both("A_log"), both("D"), scr)
        output_phase(nc, a["x"], both("out_w"), a["L0_cond_mlp_w1"], a["L0_cond_mlp_w2"], a["L0_cond_mlp_w3"],
                     mod, scr, out)


def kernel(**inputs):
    import numpy as _np
    import concourse.bacc as _bacc
    from concourse import mybir as _mybir
    from concourse.bass_utils import run_bass_kernel_spmd as _run

    nc = _bacc.Bacc("TRN2", target_bir_lowering=False, num_devices=1)
    arrays, args = {}, {}
    for name, value in inputs.items():
        v = _np.ascontiguousarray(value)
        arrays[f"in_{name}"] = v
        args[name] = nc.dram_tensor(f"in_{name}", v.shape, _mybir.dt.from_np(v.dtype), kind="ExternalInput").ap()
    out = nc.dram_tensor("out", (BATCH, SEQ, DM), fp32, kind="ExternalOutput").ap()
    build(nc, args, out)
    r = _run(nc, [arrays], core_ids=[0])
    return r.results[0]["out"]
```

```python
import concourse.bass as bass
from concourse import mybir
from contextlib import ExitStack

fp32 = mybir.dt.float32
bf16 = mybir.dt.bfloat16
ALU = mybir.AluOpType
ACT = mybir.ActivationFunctionType

BATCH, SEQ, DM = 16, 256, 256
COND = 256
DI, DS = 512, 64
MLP = 512
EPS = 1e-5
P = 128
CB = 2
CH = BATCH // CB
T = CB * SEQ
TB = T // P
MB = DM // P
CK = COND // P
JB = DI // P
DIRS = 2
PASSES = DIRS * CH
QS, GD = 4, 32
NQ, NG = DS // QS, DI // GD
GJ = P // GD
PW = DI + 2 * DS
SHIFT1, SCALE1, GATE1, SHIFT2, SCALE2, GATE2 = (MB * k for k in range(6))
NMOD = 6 * MB


def hold(sp, count, sem, value):
    sp.wait_ge(sem, value)
    sp.sem_inc(count, 1)


def identity_matrix(pool, tile, made, n):
    pool.memset(tile, 1.0).then_inc(made, 1)
    pool.wait_ge(made, n + 1)
    pool.affine_select(out=tile, in_=tile, compare_op=ALU.is_equal, fill=0.0, base=0,
                       pattern=[[-1, P]], channel_multiplier=1).then_inc(made, 1)


def project_phase(nc, x, cond, w_mod, b_mod, w_in, w_xp, dt_bias, mod, scr):
    ctx = ExitStack()
    with ctx:
        def sb(name, shape, dt=fp32):
            return ctx.enter_context(nc.sbuf_tensor(name, shape, dt))

        def sem(name):
            return ctx.enter_context(nc.semaphore(name))

        ident = sb("a_ident", [P, P])
        win = sb("a_win", [P, DIRS, MB, 2 * DI])
        wxp = sb("a_wxp", [P, DIRS, JB, PW])
        dtb = sb("a_dtb", [P, DIRS, JB])
        wmod = sb("a_wmod", [P, 2, CK, 3 * DM])
        bmod = sb("a_bmod", [P, NMOD])
        condT = sb("a_condT", [P, CK, BATCH])
        modc = sb("a_modc", [P, NMOD, CB])
        xt = sb("a_xt", [P, TB, DM])
        stats = sb("a_stats", [P, TB, 6])
        mv = sb("a_mv", [P, TB, 2])
        rvar = sb("a_rvar", [P, TB])
        rstd = sb("a_rstd", [P, TB])
        veps = sb("a_veps", [P, TB])
        xn = sb("a_xn", [P, TB, DM])
        hT = sb("a_hT", [P, DIRS, MB, T])
        xs = sb("a_xs", [P, DIRS, JB, T])
        sz = sb("a_sz", [P, JB, T])
        pre = sb("a_pre", [P, JB, T])
        ey = sb("a_ey", [P, JB, T])
        ln = sb("a_ln", [P, JB, T])
        wy = sb("a_wy", [P, JB, T])
        nd = sb("a_nd", [P, JB, T])
        dt = sb("a_dt", [P, JB, T])
        u = sb("a_u", [P, JB, T])
        bt = sb("a_bt", [P, TB, DS])
        ct = sb("a_ct", [DS, T])
        uT = sb("a_uT", [P, TB, DI])
        bank = [ctx.enter_context(nc.psum_tensor(f"a_bank{n}", [P, T], fp32)) for n in range(8)]

        sp_passed = sem("a_sp_passed")
        made = sem("a_made")
        loaded = sem("a_loaded")
        w_loaded = sem("a_w_loaded")
        mod_ps = sem("a_mod_ps")
        mod_done = sem("a_mod_done")
        x_loaded = sem("a_x_loaded")
        order = sem("a_order")
        rvar_done = sem("a_rvar_done")
        rstd_done = sem("a_rstd_done")
        xn_done = sem("a_xn_done")
        hT_done = sem("a_hT_done")
        turned_x = sem("a_turned_x")
        full = sem("a_full")
        evac = sem("a_evac")
        expln = sem("a_expln")
        dt_done = sem("a_dt_done")
        u_done = sem("a_u_done")
        st = {k: sem("a_stored_" + k) for k in ("xs", "sz", "dt", "bc", "ut")}

        XS0, Z0, UT1, DT0, B0, C0 = 2, 6, 10, 14, 18, 19
        XS1, Z1, UT0, DT1, B1, C1, JOBS = 20, 24, 28, 32, 36, 37, 38
        XS, Z, DT, BJ, CJ, UT = (XS0, XS1), (Z0, Z1), (DT0, DT1), (B0, B1), (C0, C1), (UT0, UT1)
        EV = JOBS - XS0
        X_BANK = (UT0 + TB - MB) % 8
        MISSING = TB

        def early(first, n):
            return MISSING if first and n < UT1 else 0

        def job_full(c, n, first=False):
            return c * EV + (n + early(first, n))

        def job_evac(c, n, first=False):
            return c * EV + (n - 1 + EV + early(first, n))

        def chunks(eng, body):
            body(0, True, False)
            with eng.Fori(1, CH - 1) as c:
                body(c, False, False)
            body(CH - 1, False, True)

        with nc.Block() as block:
            @block.gpsimd
            def _(pool):
                identity_matrix(pool, ident[:], made, 0)

            @block.sync
            def _(sp):
                def load_x(c):
                    sp.dma_start(xt[:, :, :],
                                 x[bass.ds(c * CB, CB), :, :].rearrange("b (h p) m -> p (b h) m", p=P)).then_inc(x_loaded, 16)

                load_x(0)
                for k in range(CK):
                    sp.dma_start(condT[:, k, :], cond[:, k * P:(k + 1) * P].rearrange("b p -> p b"),
                                 allow_slow_non_contiguous=True).then_inc(loaded, 16)
                for m in range(2):
                    sp.dma_start(wmod[:, m, :, :], w_mod[m].rearrange("(k p) n -> p k n", p=P)).then_inc(loaded, 16)
                    sp.dma_start(bmod[:, m * 3 * MB:(m + 1) * 3 * MB],
                                 b_mod[m].rearrange("(k p) -> p k", p=P), allow_slow_non_contiguous=True).then_inc(loaded, 16)
                for d in range(DIRS):
                    sp.dma_start(win[:, d, :, :], w_in[d].rearrange("(k p) n -> p k n", p=P)).then_inc(w_loaded, 16)
                    sp.dma_start(wxp[:, d, :, :], w_xp[d].rearrange("(k p) n -> p k n", p=P)).then_inc(w_loaded, 16)
                    sp.dma_start(dtb[:, d, :], dt_bias[d].rearrange("(k p) -> p k", p=P),
                                 allow_slow_non_contiguous=True).then_inc(w_loaded, 16)
                for k in st:
                    sp.sem_inc(st[k], 16)

                def put(dst, src, what):
                    sp.dma_start(dst, src).then_inc(st[what], 16)

                def rows(scratch, c, d):
                    return scratch[bass.ds(c + d * CH, 1), :, :].rearrange("a (k p) n -> p (a k) n", p=P)

                def put_x(c, d, first):
                    hold(sp, sp_passed, evac, job_evac(c, XS[d] + JB - 1, first))
                    put(rows(scr["xs"], c, d), xs[:, d, :, :], "xs")
                    hold(sp, sp_passed, evac, job_evac(c, Z[d] + JB - 1, first))
                    put(rows(scr["sz"], c, d), sz[:, :, :], "sz")

                def put_dt(c, d):
                    hold(sp, sp_passed, evac, job_evac(c, CJ[d]))
                    put(rows(scr["b"], c, d), bt[:, :, :], "bc")
                    put(scr["c"][bass.ds(c + d * CH, 1), :, :].rearrange("a s t -> s (a t)"), ct[:, :], "bc")
                    hold(sp, sp_passed, dt_done, c * DIRS + (d + 1))
                    put(rows(scr["dt"], c, d), dt[:, :, :], "dt")

                def put_ut(c, d, job):
                    hold(sp, sp_passed, evac, job)
                    put(rows(scr["ut"], c, d), uT[:, :, :], "ut")

                def body(c, first, last):
                    if not last:
                        hold(sp, sp_passed, xn_done, c + 2)
                        load_x(c + 1)
                    put_x(c, 0, first)
                    if not first:
                        put_ut(c - 1, 1, job_evac(c, UT1 + TB - 1))
                    put_dt(c, 0)
                    put_x(c, 1, first)
                    put_ut(c, 0, job_evac(c, UT0 + TB - 1))
                    put_dt(c, 1)

                chunks(sp, body)
                put_ut(CH - 1, 1, job_evac(CH - 1, JOBS + TB - 1))
                for k in ("xs", "sz", "dt", "ut"):
                    sp.wait_ge(st[k], 16 * (PASSES + 1))
                sp.wait_ge(st["bc"], 16 * (2 * PASSES + 1))

            @block.tensor
            def _(pe):
                pe.sem_inc(full, 1 + MISSING)
                pe.wait_ge(loaded, 16 * (CK + 4))
                for m in range(2):
                    for n in range(3 * MB):
                        col = (m * 3 * MB + n) * BATCH
                        for k in range(CK):
                            last = nc.tensor.matmul(bank[7][:, col:col + BATCH], wmod[:, m, k, n * P:(n + 1) * P],
                                                    condT[:, k, :], start=(k == 0), stop=(k == CK - 1))
                last.then_inc(mod_ps, 1)
                pe.wait_ge(mod_done, 1)
                pe.wait_ge(made, 2)

                def free(c, n, first):
                    if n in (X_BANK, X_BANK + 1):
                        pe.wait_ge(hT_done, c * 8 + 8)
                    elif n >= 8 + XS0:
                        before = n - 8
                        if first and UT1 <= before < UT1 + MISSING:
                            before -= 8
                        pe.wait_ge(evac, job_evac(c, before, first))
                    elif not first:
                        before = max(k for k in range(JOBS) if k % 8 == n % 8)
                        pe.wait_ge(evac, c * EV + (before - 1))

                def channels(c, job, first, weights, src, kk):
                    for j in range(JB):
                        n = job + j
                        free(c, n, first)
                        for k in range(kk):
                            last = nc.tensor.matmul(bank[n % 8][:, :], weights(k, j), src(k),
                                                    start=(k == 0), stop=(k == kk - 1))
                        last.then_inc(full, 1)

                def xz(c, d, first):
                    pe.wait_ge(hT_done, c * 8 + (6 + 2 * d))
                    channels(c, XS[d], first, lambda k, j: win[:, d, k, j * P:(j + 1) * P], lambda k: hT[:, d, k, :], MB)
                    channels(c, Z[d], first, lambda k, j: win[:, d, k, DI + j * P:DI + (j + 1) * P],
                             lambda k: hT[:, d, k, :], MB)

                def turn_x(c):
                    pe.wait_ge(xn_done, c + 2)
                    if not (isinstance(c, int) and c == 0):
                        pe.wait_ge(evac, c * EV + (UT0 + TB - 1 - 1))
                    for k in range(MB):
                        for t in range(TB):
                            turned = nc.tensor.transpose(bank[X_BANK + k][:, t * P:(t + 1) * P],
                                                         xn[:, t, k * P:(k + 1) * P], ident[:])
                        turned.then_inc(turned_x, 1)

                def dtbc(c, d, first, next_x=False):
                    pe.wait_ge(evac, job_evac(c, XS[d] + JB - 1, first))
                    channels(c, DT[d], first, lambda k, j: wxp[:, d, k, j * P:(j + 1) * P], lambda k: xs[:, d, k, :], JB)
                    if next_x:
                        turn_x(c + 1)
                    free(c, BJ[d], first)
                    for t in range(TB):
                        for k in range(JB):
                            last = nc.tensor.matmul(bank[BJ[d] % 8][:, t * DS:(t + 1) * DS],
                                                    xs[:, d, k, t * P:(t + 1) * P], wxp[:, d, k, DI:DI + DS],
                                                    start=(k == 0), stop=(k == JB - 1))
                    last.then_inc(full, 1)
                    free(c, CJ[d], first)
                    for k in range(JB):
                        last = nc.tensor.matmul(bank[CJ[d] % 8][0:DS, :], wxp[:, d, k, DI + DS:PW],
                                                xs[:, d, k, :], start=(k == 0), stop=(k == JB - 1))
                    last.then_inc(full, 1)

                def turn_u(c, job, n_u):
                    pe.wait_ge(u_done, n_u)
                    for t in range(TB):
                        n = job + t
                        free(c, n, False)
                        for j in range(JB):
                            last = nc.tensor.transpose(bank[n % 8][:, j * P:(j + 1) * P],
                                                       u[:, j, t * P:(t + 1) * P], ident[:])
                        last.then_inc(full, 1)

                def body(c, first, last):
                    if first:
                        pe.wait_ge(w_loaded, 16 * 3 * DIRS)
                    xz(c, 0, first)
                    if not first:
                        turn_u(c, UT1, c * DIRS + 1)
                    dtbc(c, 0, first)
                    xz(c, 1, first)
                    turn_u(c, UT0, c * DIRS + 2)
                    dtbc(c, 1, first, next_x=not last)

                turn_x(0)
                chunks(pe, body)
                turn_u(CH - 1, JOBS, CH * DIRS + 1)

            @block.scalar
            def _(act):
                act.sem_inc(evac, EV + MISSING)
                act.wait_ge(w_loaded, 16 * 3 * DIRS)

                def root(c):
                    act.wait_ge(rvar_done, c + 1)
                    nc.scalar.activation(rstd[:, :], rvar[:, :], ACT.Sqrt).then_inc(rstd_done, 1)

                def silu_xz(c, d, first):
                    act.wait_ge(st["xs"], (c * DIRS + (d + 1)) * 16)
                    for j in range(JB):
                        act.wait_ge(full, job_full(c, XS[d] + j, first))
                        nc.scalar.activation(xs[:, d, j, :], bank[(XS[d] + j) % 8][:, :], ACT.Silu).then_inc(evac, 1)
                    act.wait_ge(st["sz"], (c * DIRS + (d + 1)) * 16)
                    for j in range(JB):
                        act.wait_ge(full, job_full(c, Z[d] + j, first))
                        nc.scalar.activation(sz[:, j, :], bank[(Z[d] + j) % 8][:, :], ACT.Silu).then_inc(evac, 1)

                def dtbc_out(c, d, next_x=False):
                    act.wait_ge(u_done, c * DIRS + (d + 1))
                    for j in range(JB):
                        src = bank[(DT[d] + j) % 8][:, :]
                        act.wait_ge(full, job_full(c, DT[d] + j))
                        nc.scalar.activation(pre[:, j, :], src, ACT.Identity, bias=dtb[:, d, j:j + 1])
                        nc.scalar.activation(ey[:, j, :], src, ACT.Abs, bias=dtb[:, d, j:j + 1]).then_inc(evac, 1)
                    if next_x:
                        modulate(c + 1)
                    act.wait_ge(st["bc"], (c * DIRS + d) * 32 + 16)
                    act.wait_ge(full, job_full(c, BJ[d]))
                    nc.scalar.activation(bt[:, :, :], bank[BJ[d] % 8][:, 0:TB * DS].rearrange("p (t s) -> p t s", t=TB),
                                         ACT.Copy).then_inc(evac, 1)
                    act.wait_ge(full, job_full(c, CJ[d]))
                    nc.scalar.activation(ct[:, :], bank[CJ[d] % 8][0:DS, :], ACT.Copy).then_inc(evac, 1)

                def exp_ln(c, d):
                    act.wait_ge(evac, job_evac(c, DT[d] + JB - 1))
                    nc.scalar.activation(ey[:, :, :], ey[:, :, :], ACT.Exp, scale=-1.0).then_inc(expln, 1)
                    act.wait_ge(expln, c * 4 + (2 * d + 1))
                    nc.scalar.activation(ln[:, :, :], ey[:, :, :], ACT.Ln, bias=1.0).then_inc(expln, 1)

                def copy_ut(c, job, n_stored):
                    act.wait_ge(st["ut"], n_stored)
                    for t in range(TB):
                        act.wait_ge(full, job_full(c, job + t))
                        nc.scalar.activation(uT[:, t, :], bank[(job + t) % 8][:, :], ACT.Copy).then_inc(evac, 1)

                def modulate(c):
                    for k in range(MB):
                        act.wait_ge(turned_x, c * MB + (k + 1))
                        for d in range(DIRS):
                            for b in range(CB):
                                src = bank[X_BANK + k][:, b * SEQ:(b + 1) * SEQ]
                                nc.scalar.activation(hT[:, d, k, b * SEQ:(b + 1) * SEQ],
                                                     src if d == 0 else src[:, ::-1], ACT.Identity,
                                                     scale=modc[:, SCALE1 + k, b:b + 1],
                                                     bias=modc[:, SHIFT1 + k, b:b + 1]).then_inc(hT_done, 1)

                def body(c, first, last):
                    silu_xz(c, 0, first)
                    if not first:
                        copy_ut(c, UT1, c * (DIRS * 16))
                    dtbc_out(c, 0)
                    exp_ln(c, 0)
                    silu_xz(c, 1, first)
                    if not last:
                        root(c + 1)
                    copy_ut(c, UT0, c * (DIRS * 16) + 16)
                    dtbc_out(c, 1, next_x=not last)
                    exp_ln(c, 1)

                root(0)
                modulate(0)
                chunks(act, body)
                copy_ut(CH - 1, JOBS, CH * DIRS * 16)

            @block.vector
            def _(dve):
                dve.sem_inc(xn_done, 1)
                dve.sem_inc(u_done, 1)
                LN_LINKS, SP_LINKS = 3, 2

                def link(ins, n):
                    ins.then_inc(order, 1)
                    dve.wait_ge(order, n)

                def norm(c, n):
                    dve.wait_ge(x_loaded, (c + 1) * 16)
                    for t in range(TB):
                        last = nc.vector.bn_stats(stats[:, t, :], xt[:, t, :])
                    link(last, n + 1)
                    start = isinstance(c, int) and c == 0
                    if not start:
                        nc.vector.tensor_copy(modc[:, :, :], mod[:, :, bass.ds(c * CB, CB)])
                    for t in range(TB):
                        last = nc.vector.bn_aggr(mv[:, t, :], stats[:, t, :])
                    link(last, n + 2)
                    link(nc.vector.tensor_scalar(veps[:, :], mv[:, :, 1], EPS, None, ALU.add), n + 3)
                    nc.vector.reciprocal(rvar[:, :], veps[:, :]).then_inc(rvar_done, 1)
                    if start:
                        dve.wait_ge(loaded, 16 * (CK + 4))
                        dve.wait_ge(mod_ps, 1)
                        for k in range(NMOD):
                            one = 1.0 if k in (SCALE1, SCALE1 + 1, SCALE2, SCALE2 + 1) else 0.0
                            last = nc.vector.tensor_scalar(mod[:, k, :], bank[7][:, k * BATCH:(k + 1) * BATCH],
                                                           bmod[:, k:k + 1], one, ALU.add, ALU.add)
                        last.then_inc(mod_done, 1)
                        dve.wait_ge(mod_done, 1)
                        nc.vector.tensor_copy(modc[:, :, :], mod[:, :, 0:CB])
                    dve.wait_ge(rstd_done, c + 1)
                    for t in range(TB):
                        last = nc.vector.tensor_scalar(xn[:, t, :], xt[:, t, :], mv[:, t, 0:1], rstd[:, t:t + 1],
                                                       ALU.subtract, ALU.mult)
                    last.then_inc(xn_done, 1)

                def softplus(c, d, n):
                    dve.wait_ge(expln, c * 4 + (2 * d + 1))
                    link(nc.vector.tensor_scalar(wy[:, :, :], ey[:, :, :], 1.0, None, ALU.add), n + 1)
                    nc.vector.scalar_tensor_tensor(out=nd[:, :, :], in0=wy[:, :, :], scalar=-1.0, in1=ey[:, :, :],
                                                   op0=ALU.add, op1=ALU.subtract)
                    dve.wait_ge(expln, c * 4 + (2 * d + 2))
                    link(nc.vector.scalar_tensor_tensor(out=ln[:, :, :], in0=pre[:, :, :], scalar=0.0, in1=ln[:, :, :],
                                                        op0=ALU.max, op1=ALU.add), n + 2)
                    dve.wait_ge(st["dt"], (c * DIRS + (d + 1)) * 16)
                    nc.vector.tensor_tensor(dt[:, :, :], ln[:, :, :], nd[:, :, :], ALU.subtract).then_inc(dt_done, 1)
                    dve.wait_ge(dt_done, c * DIRS + (d + 1))

                def body(c, first, last):
                    n = c * (LN_LINKS + 2 * SP_LINKS) + LN_LINKS
                    softplus(c, 0, n)
                    if not first:
                        dve.wait_ge(full, job_full(c, UT1 + TB - 1))
                    nc.vector.tensor_tensor(u[:, :, :], dt[:, :, :], xs[:, 0, :, :], ALU.mult).then_inc(u_done, 1)
                    n = n + SP_LINKS
                    if not last:
                        norm(c + 1, n)
                        n = n + LN_LINKS
                    softplus(c, 1, n)
                    dve.wait_ge(full, job_full(c, UT0 + TB - 1))
                    nc.vector.tensor_tensor(u[:, :, :], dt[:, :, :], xs[:, 1, :, :], ALU.mult).then_inc(u_done, 1)

                norm(0, 0)
                chunks(dve, body)


def scan_phase(nc, a_log, d_skip, scr):
    ctx = ExitStack()
    with ctx:
        def sb(name, shape, dt=fp32):
            return ctx.enter_context(nc.sbuf_tensor(name, shape, dt))

        def pb(name):
            return ctx.enter_context(nc.psum_tensor(name, [P, T], fp32))

        def sem(name):
            return ctx.enter_context(nc.semaphore(name))

        NDA = 8
        UPQ = NG
        UPP = NQ * UPQ
        GPQ = UPQ // GJ
        VPQ = GPQ - 1
        SPB = GJ // 2
        NPROD = TB * QS
        ACT_PRODUCTS = tuple(zip(range(7), (2, 4, 5, 7, 9, 11, 12)))
        DVE_PRODUCTS = tuple(zip((*range(8, NPROD), 7), (0, 1, 1, 2, 3, 3, 4, 5, 5)))
        PPA, PPD = len(ACT_PRODUCTS), len(DVE_PRODUCTS)
        assert sorted(n for n, at in ACT_PRODUCTS + DVE_PRODUCTS) == list(range(NPROD))
        LOAD = QS * 16

        ident = sb("b_ident", [P, P])
        summer = sb("b_summer", [P, GD])
        zero = sb("b_zero", [P, T], bf16)
        negA = sb("b_negA", [P, DIRS, NG, NQ])
        dskip = sb("b_dskip", [P, DIRS, JB])
        dtr = sb("b_dtr", [P, NG, T])
        uT = sb("b_uT", [P, TB, DI])
        bt = sb("b_bt", [P, TB, DS])
        crep = sb("b_crep", [P, 2, T])
        ub = sb("b_ub", [P, 2, TB, NG, QS, GD])
        dA = sb("b_dA", [P, NDA, CB, SEQ])
        hc = sb("b_hc", [P, NG, T])
        xs = sb("b_xs", [P, JB, T])
        y = [pb(f"b_y{j}") for j in range(JB)]
        pair_in = [ctx.enter_context(nc.psum_tensor(f"b_in{e}", [P, 2, T], fp32)) for e in range(SPB)]

        sp_passed = sem("b_sp_passed")
        made = sem("b_made")
        loaded = sem("b_loaded")
        a_exp = sem("b_a_exp")
        a_done = sem("b_a_done")
        cleared = sem("b_cleared")
        dt_loaded = [sem(f"b_dt_loaded{j}") for j in range(JB)]
        ut_loaded = [sem(f"b_ut_loaded{t}") for t in range(TB)]
        c_loaded = [sem("b_c_loaded0"), sem("b_c_loaded1")]
        xs_loaded = sem("b_xs_loaded")
        prod_act = sem("b_prod_act")
        prod_dve = sem("b_prod_dve")
        exp_done = sem("b_exp_done")
        turned = [sem(f"b_turned{e}") for e in range(SPB)]
        scanned = sem("b_scanned")
        hc_pool = sem("b_hc_pool")
        hc_dve = sem("b_hc_dve")
        summed = sem("b_summed")
        y_read = sem("b_y_read")
        stored = sem("b_stored")

        SCANS0 = SPB * (NDA // GJ)

        H = NQ // 2

        def passes(eng, one_pass, direction=False):
            if not direction:
                one_pass(0, 0, True, False)
                with eng.Fori(1, PASSES - 1) as p:
                    one_pass(p, None, False, False)
                one_pass(PASSES - 1, None, False, True)
                return
            one_pass(0, 0, True, False)
            with eng.Fori(1, CH) as c:
                one_pass(c, 0, False, False)
            with eng.Fori(0, CH - 1) as c:
                one_pass(c + CH, 1, False, False)
            one_pass(PASSES - 1, 1, False, True)

        def halves(eng, half_pass):
            half_pass(0, True, False)
            with eng.Fori(1, H - 1) as half:
                half_pass(half, False, False)
            half_pass(H - 1, False, True)

        with nc.Block() as block:
            @block.sync
            def _(sp):
                def one(scratch, p):
                    return scratch[bass.ds(p, 1), :, :]

                def rows(scratch, p):
                    return one(scratch, p).rearrange("a (k p) n -> p (a k) n", p=P)

                U_ORDER = (0, 2, 3, 1)

                def load_u(p, t):
                    for dst, src in ((uT, scr["ut"]), (bt, scr["b"])):
                        sp.dma_start(dst[:, t, :], one(src, p)[:, t * P:(t + 1) * P, :]
                                     .rearrange("a p n -> p (a n)")).then_inc(ut_loaded[t], 16)

                def load_dt(p, j):
                    for i in range(QS):
                        sp.dma_start(dtr[i * GD:(i + 1) * GD, j * GJ:(j + 1) * GJ, :],
                                     one(scr["dt"], p)[:, j * P:(j + 1) * P, :]
                                     .rearrange("a (g d) t -> d (a g) t", d=GD)).then_inc(dt_loaded[j], 16)

                def load_c(p, q, k):
                    for i in range(QS):
                        sp.dma_start(crep[i * GD:(i + 1) * GD, k, :],
                                     one(scr["c"], p)[:, bass.ds(q + (i * NQ + k), 1), :]
                                     .rearrange("a s t -> (a s) t").broadcast_to((GD, T))).then_inc(c_loaded[k], 16)

                def c_used(n):
                    hold(sp, sp_passed, hc_pool, (n + 1) * GPQ + 1)
                    hold(sp, sp_passed, hc_dve, (n + 1) * VPQ + 1)

                for t in U_ORDER:
                    load_u(0, t)
                load_c(0, 0, 0)
                for j in range(JB):
                    load_dt(0, j)
                load_c(0, 0, 1)

                def one_pass(p, d, first, last):
                    if not first:
                        hold(sp, sp_passed, y_read, p * JB + JB)
                        sp.dma_start(rows(scr["y"], p - 1), xs[:, :, :]).then_inc(stored, 16)
                        hold(sp, sp_passed, stored, p * 16)
                    sp.dma_start(xs[:, :, :], rows(scr["xs"], p)).then_inc(xs_loaded, 16)
                    with sp.Fori(1, H) as half:
                        for k in range(2):
                            c_used((p * NQ + half * 2) + (k - 2))
                            load_c(p, half * 2, k)
                    if not last:
                        for t in U_ORDER:
                            for count, order in ((prod_act, ACT_PRODUCTS), (prod_dve, DVE_PRODUCTS)):
                                readers = [m + 1 for m, (n, at) in enumerate(order) if n // QS == t]
                                if readers:
                                    hold(sp, sp_passed, count,
                                         p * (NQ * len(order)) + ((NQ - 1) * len(order) + readers[-1]))
                            load_u(p + 1, t)
                        for j in range(JB):
                            if j == JB // 2:
                                c_used(p * NQ + (NQ - 2))
                                load_c(p + 1, 0, 0)
                            hold(sp, sp_passed, exp_done, p * UPP + (UPP - UPQ + (j + 1) * GJ + 1))
                            load_dt(p + 1, j)
                        c_used(p * NQ + (NQ - 1))
                        load_c(p + 1, 0, 1)

                passes(sp, one_pass)
                sp.wait_ge(y_read, PASSES * JB + JB)
                sp.dma_start(scr["y"][PASSES - 1].rearrange("(k p) n -> p k n", p=P), xs[:, :, :]).then_inc(stored, 16)
                sp.wait_ge(stored, 16 * PASSES)

            @block.gpsimd
            def _(pool):
                identity_matrix(pool, ident[:], made, 0)
                pool.memset(summer[:], 0.0).then_inc(made, 1)
                for i in range(QS):
                    pool.wait_ge(made, 3 + i)
                    pool.affine_select(out=summer[:], in_=summer[:], compare_op=ALU.not_equal, fill=1.0, base=-i * GD,
                                       pattern=[[-1, GD]], channel_multiplier=1).then_inc(made, 1)
                pool.memset(zero[:], 0.0).then_inc(made, 1)
                pool.sem_inc(hc_pool, 1)

                def quad(p, half, k):
                    B = (p * NQ + half * 2) * GPQ
                    pool.wait_ge(c_loaded[k], (p * H + half + 1) * LOAD)
                    for j in range(GPQ):
                        units = GJ if j == GPQ - 1 else GJ - 1
                        mine = slice(j * GJ, j * GJ + units)
                        pool.wait_ge(scanned, B * SPB + ((k * GPQ + j) * SPB + SPB + SCANS0))
                        nc.gpsimd.tensor_tensor(hc[:, mine, :], hc[:, mine, :],
                                                crep[:, k:k + 1, :].broadcast_to((P, units, T)), ALU.mult).then_inc(hc_pool, 1)

                with pool.Fori(0, PASSES) as p:
                    with pool.Fori(0, H) as half:
                        quad(p, half, 0)
                        quad(p, half, 1)

            @block.scalar
            def _(act):
                for d in range(DIRS):
                    for i in range(QS):
                        act.dma_start(negA[i * GD:(i + 1) * GD, d, :, :],
                                      a_log[d][:, i * NQ:(i + 1) * NQ]
                                      .rearrange("(g d) q -> d g q", d=GD)).then_inc(loaded, 16)
                    act.dma_start(dskip[:, d, :], d_skip[d].rearrange("(k p) -> p k", p=P),
                                  allow_slow_non_contiguous=True).then_inc(loaded, 16)
                act.sem_inc(exp_done, 1)
                act.wait_ge(loaded, 16 * DIRS * (QS + 1))
                nc.scalar.activation(negA[:, :, :, :], negA[:, :, :, :], ACT.Exp).then_inc(a_exp, 1)
                act.wait_ge(a_done, 1)
                act.wait_ge(cleared, 1)

                def product(n, k, col):
                    t, i = divmod(n, QS)
                    nc.scalar.activation(ub[:, k, t, :, i, :], uT[:, t, :].rearrange("p (g d) -> p g d", g=NG),
                                         ACT.Copy, scale=bt[:, t, bass.ds(col + i * NQ, 1)]).then_inc(prod_act, 1)

                def quad(p, d, half, k, first, wrap, nxt):
                    B = (p * NQ + half * 2) * GPQ
                    for g in range(UPQ):
                        if first and g % GJ == 0:
                            act.wait_ge(dt_loaded[g // GJ], (p + 1) * LOAD)
                        if g % 2 == 0:
                            act.wait_ge(scanned, B * SPB + (k * GPQ * SPB + g // 2 + 1))
                        nc.scalar.activation(dA[:, g % NDA, :, 1:SEQ],
                                             dtr[:, g, :].rearrange("p (b t) -> p b t", b=CB)[:, :, 1:SEQ], ACT.Exp,
                                             scale=negA[:, d, g, bass.ds(half * 2 + k, 1)]).then_inc(exp_done, 1)
                        for m, (n, at) in enumerate(ACT_PRODUCTS):
                            if nxt and at == g:
                                if m == 0:
                                    act.wait_ge(turned[-1], B + (k * GPQ + 1))
                                if wrap:
                                    act.wait_ge(ut_loaded[n // QS], (p + 2) * 32)
                                product(n, (k + 1) % 2, 0 if wrap else half * 2 + (k + 1))

                def one_pass(p, d, first, last):
                    def half_pass(half, h_first, h_last):
                        quad(p, d, half, 0, h_first, False, True)
                        quad(p, d, half, 1, False, h_last, not (h_last and last))

                    halves(act, half_pass)

                for n, at in ACT_PRODUCTS:
                    act.wait_ge(ut_loaded[n // QS], 32)
                    product(n, 0, 0)
                passes(act, one_pass, direction=True)

            @block.vector
            def _(dve):
                dve.sem_inc(scanned, SCANS0)
                dve.sem_inc(hc_dve, 1)
                dve.sem_inc(y_read, JB)
                nc.vector.memset(dA[:, :, :, 0:1], 0.0).then_inc(cleared, 1)
                dve.wait_ge(a_exp, 1)
                nc.vector.tensor_scalar(negA[:, :, :, :], negA[:, :, :, :], -1.0, None, ALU.mult).then_inc(a_done, 1)
                dve.wait_ge(cleared, 1)

                def product(n, k, col):
                    t, i = divmod(n, QS)
                    nc.vector.tensor_scalar(ub[:, k, t, :, i, :], uT[:, t, :].rearrange("p (g d) -> p g d", g=NG),
                                            bt[:, t, bass.ds(col + i * NQ, 1)], None, ALU.mult).then_inc(prod_dve, 1)

                def times_c(p, half, k, j):
                    B = (p * NQ + half * 2) * GPQ
                    if j == 0:
                        dve.wait_ge(c_loaded[k], (p * H + half + 1) * LOAD)
                    dve.wait_ge(scanned, B * SPB + ((k * GPQ + j + 1) * SPB + SCANS0))
                    mine = hc[:, j * GJ + GJ - 1, :]
                    nc.vector.tensor_tensor(mine, mine, crep[:, k, :], ALU.mult).then_inc(hc_dve, 1)

                def read_y(p, d, j):
                    if j == 0:
                        dve.wait_ge(xs_loaded, (p + 1) * 16)
                    dve.wait_ge(summed, (p + 1) * (NQ * GPQ) - (JB - 1 - j) + GPQ)
                    nc.vector.scalar_tensor_tensor(out=xs[:, j, :], in0=xs[:, j, :], scalar=dskip[:, d, j:j + 1],
                                                   in1=y[j][:, :], op0=ALU.mult, op1=ALU.add).then_inc(y_read, 1)

                def quad(p, half, k, wrap, nxt, read_before):
                    B = (p * NQ + half * 2) * GPQ
                    U = (p * NQ + half * 2) * UPQ

                    def scan(j, e):
                        g = j * GJ + 2 * e
                        dve.wait_ge(exp_done, U + (k * UPQ + g + 2 + 1))
                        dve.wait_ge(turned[e], B + (k * GPQ + j + 1 + 1))
                        nc.vector.tensor_tensor_scan(hc[:, g:g + 2, :].rearrange("p n t -> p (n t)"),
                                                     dA[:, g % NDA:g % NDA + 2, :, :].rearrange("p n b t -> p (n b t)"),
                                                     pair_in[e][:, :, :].rearrange("p n t -> p (n t)"), 0.0,
                                                     ALU.mult, ALU.add).then_inc(scanned, 1)

                    def between(at):
                        for m, (n, after) in enumerate(DVE_PRODUCTS):
                            if nxt and after == at:
                                if m == 0:
                                    dve.wait_ge(turned[-1], B + (k * GPQ + 1))
                                if wrap:
                                    dve.wait_ge(ut_loaded[n // QS], (p + 2) * 32)
                                product(n, (k + 1) % 2, 0 if wrap else half * 2 + (k + 1))
                        if read_before is not None and at >= SPB * GPQ - JB:
                            read_y(p - 1, read_before, at - (SPB * GPQ - JB))

                    for j in range(GPQ):
                        dve.wait_ge(summed, B + (k * GPQ + j + 1))
                        scan(j, 0)
                        if j:
                            times_c(p, half, k, j - 1)
                        between(j * SPB)
                        scan(j, 1)
                        between(j * SPB + 1)

                def one_pass(p, d, first, last, d_before):
                    def half_pass(half, h_first, h_last):
                        quad(p, half, 0, False, True, d_before if h_first else None)
                        quad(p, half, 1, h_last, not (h_last and last), None)

                    halves(dve, half_pass)

                for n, at in DVE_PRODUCTS:
                    dve.wait_ge(ut_loaded[n // QS], 32)
                    product(n, 0, 0)
                one_pass(0, 0, True, False, None)
                with dve.Fori(1, CH + 1) as p:
                    one_pass(p, None, False, False, 0)
                with dve.Fori(CH + 1, PASSES - 1) as p:
                    one_pass(p, None, False, False, 1)
                one_pass(PASSES - 1, None, False, True, 1)
                for j in range(JB):
                    read_y(PASSES - 1, 1, j)

            @block.tensor
            def _(pe):
                for e in range(SPB):
                    pe.sem_inc(turned[e], 1)
                pe.sem_inc(summed, GPQ)
                pe.wait_ge(made, 3 + QS + 1)

                def turn(Q, k, j, e):
                    k, j = k + j // GPQ, j % GPQ
                    if j == 0 and e == 0:
                        pe.wait_ge(prod_act, Q * PPA + (k + 1) * PPA)
                        pe.wait_ge(prod_dve, Q * PPD + (k + 1) * PPD)
                    pe.wait_ge(scanned, Q * (GPQ * SPB) + ((k * GPQ + j - 1) * SPB + e + 1 + SCANS0))
                    for n in range(2):
                        for t in range(TB):
                            last = nc.tensor.transpose(pair_in[e][:, n, t * P:(t + 1) * P],
                                                       ub[:, k % 2, t, j * GJ + 2 * e + n, :, :]
                                                       .rearrange("p i d -> p (i d)"), ident[:])
                    last.then_inc(turned[e], 1)

                def add(p, Q, n, start, stop):
                    j = n % GPQ
                    if start:
                        pe.wait_ge(y_read, p * JB + (j + 1))
                        nc.tensor.matmul(y[j][:, :], zero[:, 0:P], zero[:, :], start=True, stop=False,
                                         skip_group_check=True)
                    pe.wait_ge(hc_pool, Q * GPQ + (n + 1 + 1))
                    if j < VPQ:
                        pe.wait_ge(hc_dve, Q * VPQ + (n // GPQ * VPQ + j + 1 + 1))
                    for e in range(GJ):
                        last = nc.tensor.matmul(y[j][e * GD:(e + 1) * GD, :], summer[:, :], hc[:, j * GJ + e, :],
                                                start=False, stop=stop, tile_position=(0, e * GD), skip_group_check=True)
                    last.then_inc(summed, 1)

                LAG = 2

                def one_pass(p, d, first, last):
                    def half_pass(half, h_first, h_last):
                        Q = p * NQ + half * 2
                        for k in range(2):
                            for j in range(GPQ):
                                end = h_last and last and k == 1 and j == GPQ - 1
                                if not end:
                                    turn(Q, k, j + 1, 0)
                                n = k * GPQ + j - LAG
                                if not (first and h_first and n < 0):
                                    add(p, Q, n, h_first and 0 <= n < GPQ,
                                        (h_first and n < 0) or (h_last and n >= GPQ))
                                if not end:
                                    turn(Q, k, j + 1, 1)

                    halves(pe, half_pass)

                for e in range(SPB):
                    turn(0, 0, 0, e)
                passes(pe, one_pass)
                for n in range(2 * GPQ - LAG, 2 * GPQ):
                    add(PASSES - 1, PASSES * NQ - 2, n, False, True)


def output_phase(nc, x, w_out, w1, w2, w3, mod, scr, out):
    ctx = ExitStack()
    with ctx:
        def sb(name, shape, dt=fp32):
            return ctx.enter_context(nc.sbuf_tensor(name, shape, dt))

        def sem(name):
            return ctx.enter_context(nc.semaphore(name))

        ident = sb("c_ident", [P, P])
        mean_w = sb("c_mean_w", [P, P])
        wo = sb("c_wo", [P, DIRS, JB, DM])
        w1s = sb("c_w1", [P, MB, MLP])
        w2s = sb("c_w2", [P, MB, MLP])
        w3s = sb("c_w3", [P, JB, DM])
        modc = sb("c_modc", [P, NMOD, CB])
        xt = sb("c_xt", [P, TB, DM])
        gs = sb("c_gs", [P, DIRS, JB, T])
        sz = sb("c_sz", [P, DIRS, JB, T])
        of = sb("c_of", [P, MB, T])
        x1 = sb("c_x1", [P, MB, T])
        xc = sb("c_xc", [P, MB, T])
        sq = sb("c_sq", [P, MB, T])
        ve = sb("c_ve", [P, T])
        rv = sb("c_rv", [P, T])
        rs = sb("c_rs", [P, T])
        xm = sb("c_xm", [P, MB, T])
        h2 = sb("c_h2", [P, MB, T])
        gate = sb("c_gate", [P, JB, T])
        x2 = sb("c_x2", [P, MB, T])
        ot = sb("c_ot", [P, TB, DM])
        x1_held = sb("c_x1_held", [P, MB, T])
        gate_held = sb("c_gate_held", [P, MB, CB])
        bank = [ctx.enter_context(nc.psum_tensor(f"c_bank{n}", [P, T], fp32)) for n in range(8)]
        OF, OB, XT, MEAN, VAR, FRONT_JOBS = 0, 2, 4, 6, 7, 8
        UP, DOWN, OUT, BACK_JOBS = 0, 8, 10, 12
        front_bank = (0, 1, 2, 3, 4, 5, 6, 7)
        back_bank = (6, 7, 0, 1, 2, 3, 4, 5, 0, 1, 4, 5)

        sp_passed = sem("c_sp_passed")
        made = sem("c_made")
        wo_loaded = sem("c_wo_loaded")
        mlp_loaded = sem("c_mlp_loaded")
        y_loaded = [sem("c_y_loaded0"), sem("c_y_loaded1")]
        x_loaded = sem("c_x_loaded")
        gated = sem("c_gated")
        front_full = sem("c_front_full")
        back_full = sem("c_back_full")
        of_done = sem("c_of_done")
        order = sem("c_order")
        x1_done = sem("c_x1_done")
        x1_kept = sem("c_x1_kept")
        xc_done = sem("c_xc_done")
        sq_done = sem("c_sq_done")
        rv_done = sem("c_rv_done")
        rs_done = sem("c_rs_done")
        h2_done = sem("c_h2_done")
        silu_done = sem("c_silu_done")
        gate_done = sem("c_gate_done")
        x2_done = sem("c_x2_done")
        copied = sem("c_copied")
        stored = sem("c_stored")

        def front_job(f, n):
            return f * FRONT_JOBS + (n + 1)

        def back_job(b, n):
            return b * BACK_JOBS + (n + 1)

        with nc.Block() as block:
            @block.gpsimd
            def _(pool):
                identity_matrix(pool, ident[:], made, 0)
                pool.memset(mean_w[:], 1.0 / DM).then_inc(made, 1)
                with pool.Fori(0, CH) as f:
                    for d in (1, 0):
                        pool.wait_ge(y_loaded[d], (f + 1) * 32)
                        nc.gpsimd.tensor_tensor(gs[:, d, :, :], gs[:, d, :, :], sz[:, d, :, :], ALU.mult).then_inc(gated, 1)

            @block.sync
            def _(sp):
                def load_y(f, d):
                    for dst, src in ((gs, scr["y"]), (sz, scr["sz"])):
                        sp.dma_start(dst[:, d, :, :], src[bass.ds(f + d * CH, 1), :, :]
                                     .rearrange("a (k p) n -> p (a k) n", p=P)).then_inc(y_loaded[d], 16)

                def load_x(f):
                    sp.dma_start(xt[:, :, :], x[bass.ds(f * CB, CB), :, :]
                                 .rearrange("b (h p) m -> p (b h) m", p=P)).then_inc(x_loaded, 16)

                for d in (1, 0):
                    load_y(0, d)
                    sp.dma_start(wo[:, d, :, :], w_out[d].rearrange("(k p) n -> p k n", p=P)).then_inc(wo_loaded, 16)
                load_x(0)
                for dst, src in ((w1s, w1), (w2s, w2), (w3s, w3)):
                    sp.dma_start(dst[:, :, :], src.rearrange("(k p) n -> p k n", p=P)).then_inc(mlp_loaded, 16)
                with sp.Fori(0, CH - 1) as c:
                    hold(sp, sp_passed, front_full, front_job(c, MB - 1))
                    load_y(c + 1, 1)
                    hold(sp, sp_passed, front_full, front_job(c, XT - 1))
                    load_y(c + 1, 0)
                    hold(sp, sp_passed, front_full, front_job(c, XT + MB - 1))
                    load_x(c + 1)

            @block.tensor
            def _(pe):
                def front_products(f):
                    for d in (1, 0):
                        pe.wait_ge(gated, f * DIRS + (DIRS - d))
                        for m in range(MB):
                            n = (OF, OB)[d] + m
                            for k in range(JB):
                                last = nc.tensor.matmul(bank[front_bank[n]][:, :], wo[:, d, k, m * P:(m + 1) * P],
                                                        gs[:, d, k, :], start=(k == 0), stop=(k == JB - 1))
                            last.then_inc(front_full, 1)
                    if not isinstance(f, int):
                        pe.wait_ge(copied, f * 2 + (1 - 2))
                    pe.wait_ge(x_loaded, (f + 1) * 16)
                    for m in range(MB):
                        for t in range(TB):
                            last = nc.tensor.transpose(bank[front_bank[XT + m]][:, t * P:(t + 1) * P],
                                                       xt[:, t, m * P:(m + 1) * P], ident[:])
                        last.then_inc(front_full, 1)

                def over_channels(src, n):
                    for m in range(MB):
                        last = nc.tensor.matmul(bank[front_bank[n]][:, :], mean_w[:], src[:, m, :],
                                                start=(m == 0), stop=(m == MB - 1))
                    last.then_inc(front_full, 1)

                def up(j):
                    for e, w in enumerate((w1s, w2s)):
                        for k in range(MB):
                            last = nc.tensor.matmul(bank[back_bank[UP + 2 * j + e]][:, :], w[:, k, j * P:(j + 1) * P],
                                                    h2[:, k, :], start=(k == 0), stop=(k == MB - 1))
                        last.then_inc(back_full, 1)

                def down_and_out(b):
                    pe.wait_ge(gate_done, (b + 1) * JB)
                    for m in range(MB):
                        for k in range(JB):
                            last = nc.tensor.matmul(bank[back_bank[DOWN + m]][:, :], w3s[:, k, m * P:(m + 1) * P],
                                                    gate[:, k, :], start=(k == 0), stop=(k == JB - 1))
                        last.then_inc(back_full, 1)
                    pe.wait_ge(x2_done, b + 1)
                    for t in range(TB):
                        for m in range(MB):
                            last = nc.tensor.transpose(
                                bank[back_bank[OUT + t // 2]][:, (t % 2 * MB + m) * P:(t % 2 * MB + m + 1) * P],
                                x2[:, m, t * P:(t + 1) * P], ident[:])
                        if t % 2:
                            last.then_inc(back_full, 1)

                pe.wait_ge(made, 3)
                pe.wait_ge(wo_loaded, 16 * DIRS)
                front_products(0)
                pe.wait_ge(x1_done, 1)
                over_channels(x1, MEAN)
                pe.wait_ge(sq_done, 1)
                over_channels(sq, VAR)
                pe.wait_ge(mlp_loaded, 16 * 3)
                with pe.Fori(0, CH - 1) as c:
                    front_products(c + 1)
                    pe.wait_ge(h2_done, c + 1)
                    up(0)
                    pe.wait_ge(of_done, c + 2)
                    up(1)
                    pe.wait_ge(x1_done, c + 2)
                    up(2)
                    pe.wait_ge(gate_done, c * JB + 1)
                    over_channels(x1, MEAN)
                    up(3)
                    pe.wait_ge(sq_done, c + 2)
                    over_channels(sq, VAR)
                    down_and_out(c)
                pe.wait_ge(h2_done, CH)
                for j in range(JB - 1):
                    up(j)
                pe.wait_ge(copied, (CH - 1) * 2 + 1)
                up(JB - 1)
                down_and_out(CH - 1)

            @block.scalar
            def _(act):
                def copy_of(f):
                    for m in range(MB):
                        act.wait_ge(front_full, front_job(f, XT - MB + m))
                        last = nc.scalar.activation(of[:, m, :], bank[front_bank[OF + m]][:, :], ACT.Copy)
                    last.then_inc(of_done, 1)

                def silu(b, j):
                    act.wait_ge(back_full, back_job(b, UP + 2 * j))
                    nc.scalar.activation(gate[:, j, :], bank[back_bank[UP + 2 * j]][:, :], ACT.Silu).then_inc(silu_done, 1)

                def square(f):
                    act.wait_ge(xc_done, f + 1)
                    nc.scalar.activation(sq[:, :, :], xc[:, :, :], ACT.Square).then_inc(sq_done, 1)

                def root(f):
                    act.wait_ge(rv_done, f + 1)
                    nc.scalar.activation(rs[:, :], rv[:, :], ACT.Sqrt).then_inc(rs_done, 1)

                def keep_x1(f):
                    act.wait_ge(x1_done, f + 1)
                    nc.scalar.activation(x1_held[:, :, :], x1[:, :, :], ACT.Copy).then_inc(x1_kept, 1)

                def store(b):
                    act.wait_ge(stored, (b + 1) * 16)
                    for e in range(2):
                        act.wait_ge(back_full, back_job(b, OUT + e))
                        nc.scalar.activation(ot[:, 2 * e:2 * e + 2, :],
                                             bank[back_bank[OUT + e]][:, :].rearrange("p (t m) -> p t m", t=2),
                                             ACT.Copy).then_inc(copied, 1)
                    act.wait_ge(copied, b * 2 + 3)
                    act.dma_start(out[bass.ds(b * CB, CB), :, :].rearrange("b (h p) m -> p (b h) m", p=P),
                                  ot[:, :, :]).then_inc(stored, 16)

                act.sem_inc(copied, 1)
                act.sem_inc(stored, 16)
                copy_of(0)
                square(0)
                root(0)
                keep_x1(0)
                with act.Fori(0, CH - 1) as c:
                    copy_of(c + 1)
                    for j in range(JB - 1):
                        silu(c, j)
                    square(c + 1)
                    silu(c, JB - 1)
                    root(c + 1)
                    store(c)
                    keep_x1(c + 1)
                for j in range(JB):
                    silu(CH - 1, j)
                store(CH - 1)
                act.wait_ge(stored, (CH + 1) * 16)

            @block.vector
            def _(dve):
                LINKS = 3
                chain = [0]

                def link(ins, f):
                    chain[0] += 1
                    ins.then_inc(order, 1)
                    dve.wait_ge(order, f * LINKS + ((chain[0] - 1) % LINKS + 1))

                def per_batch(ap, b):
                    return ap[:, b * SEQ:(b + 1) * SEQ]

                def first_residual(f):
                    dve.wait_ge(of_done, f + 1)
                    if not isinstance(f, int):
                        dve.wait_ge(h2_done, f)
                    nc.vector.tensor_copy(modc[:, :, :], mod[:, :, bass.ds(f * CB, CB)])
                    for m in range(MB):
                        for b in range(CB):
                            last = nc.vector.tensor_tensor(per_batch(of[:, m, :], b), per_batch(of[:, m, :], b),
                                                           per_batch(bank[front_bank[OB + m]][:, :], b)[:, ::-1], ALU.add)
                    link(last, f)
                    dve.wait_ge(front_full, front_job(f, XT + MB - 1))
                    if not isinstance(f, int):
                        dve.wait_ge(x1_kept, f)
                        nc.vector.tensor_copy(gate_held[:, :, :], mod[:, GATE2:GATE2 + MB, bass.ds(f * CB + (0 - CB), CB)])
                    for m in range(MB):
                        for b in range(CB):
                            last = nc.vector.scalar_tensor_tensor(
                                out=per_batch(x1[:, m, :], b), in0=per_batch(of[:, m, :], b),
                                scalar=modc[:, GATE1 + m, b:b + 1], in1=per_batch(bank[front_bank[XT + m]][:, :], b),
                                op0=ALU.mult, op1=ALU.add)
                    last.then_inc(x1_done, 1)

                def center(f):
                    dve.wait_ge(front_full, front_job(f, MEAN))
                    for m in range(MB):
                        last = nc.vector.tensor_tensor(xc[:, m, :], x1[:, m, :], bank[front_bank[MEAN]][:, :], ALU.subtract)
                    last.then_inc(xc_done, 1)

                def modulate(f):
                    dve.wait_ge(front_full, front_job(f, VAR))
                    link(nc.vector.tensor_scalar(ve[:, :], bank[front_bank[VAR]][:, :], EPS, None, ALU.add), f)
                    nc.vector.reciprocal(rv[:, :], ve[:, :]).then_inc(rv_done, 1)
                    dve.wait_ge(rs_done, f + 1)
                    for m in range(MB):
                        last = nc.vector.tensor_tensor(xm[:, m, :], xc[:, m, :], rs[:, :], ALU.mult)
                    link(last, f)
                    for m in range(MB):
                        for b in range(CB):
                            last = nc.vector.tensor_scalar(per_batch(h2[:, m, :], b), per_batch(xm[:, m, :], b),
                                                           modc[:, SCALE2 + m, b:b + 1], modc[:, SHIFT2 + m, b:b + 1],
                                                           ALU.mult, ALU.add)
                    last.then_inc(h2_done, 1)

                def gated(b, j):
                    dve.wait_ge(silu_done, b * JB + (j + 1))
                    dve.wait_ge(back_full, back_job(b, UP + 2 * j + 1))
                    nc.vector.tensor_tensor(gate[:, j, :], gate[:, j, :], bank[back_bank[UP + 2 * j + 1]][:, :],
                                            ALU.mult).then_inc(gate_done, 1)

                def second_residual(c):
                    dve.wait_ge(x1_kept, c + 1)
                    dve.wait_ge(back_full, back_job(c, DOWN + MB - 1))
                    for m in range(MB):
                        for b in range(CB):
                            last = nc.vector.scalar_tensor_tensor(
                                out=per_batch(x2[:, m, :], b), in0=per_batch(bank[back_bank[DOWN + m]][:, :], b),
                                scalar=gate_held[:, m, b:b + 1], in1=per_batch(x1_held[:, m, :], b),
                                op0=ALU.mult, op1=ALU.add)
                    last.then_inc(x2_done, 1)

                first_residual(0)
                center(0)
                modulate(0)
                with dve.Fori(0, CH - 1) as c:
                    first_residual(c + 1)
                    for j in range(MB):
                        gated(c, j)
                    center(c + 1)
                    for j in range(MB, JB):
                        gated(c, j)
                    modulate(c + 1)
                    second_residual(c)
                dve.wait_ge(x2_done, CH - 1)
                nc.vector.tensor_copy(gate_held[:, :, :], mod[:, GATE2:GATE2 + MB, (CH - 1) * CB:CH * CB])
                for j in range(JB):
                    gated(CH - 1, j)
                second_residual(CH - 1)


def build(nc, a, out):
    scr = {k: nc.dram_tensor("scratch_" + k, [PASSES, DI, T], fp32).ap() for k in ("xs", "sz", "dt", "y")}
    scr["ut"] = nc.dram_tensor("scratch_ut", [PASSES, T, DI], fp32).ap()
    scr["b"] = nc.dram_tensor("scratch_b", [PASSES, T, DS], fp32).ap()
    scr["c"] = nc.dram_tensor("scratch_c", [PASSES, DS, T], fp32).ap()
    both = lambda name: [a[f"L0_cond_{d}_{name}"] for d in ("fwd", "bwd")]
    with nc.sbuf_tensor("mod", [P, NMOD, BATCH], fp32) as mod:
        project_phase(nc, a["x"], a["cond_1024"], [a["L0_cond_adaln_mamba_w"], a["L0_cond_adaln_mlp_w"]],
                      [a["L0_cond_adaln_mamba_b"], a["L0_cond_adaln_mlp_b"]], both("in_w"), both("xproj_w"),
                      both("dt_bias"), mod, scr)
        scan_phase(nc, both("A_log"), both("D"), scr)
        output_phase(nc, a["x"], both("out_w"), a["L0_cond_mlp_w1"], a["L0_cond_mlp_w2"], a["L0_cond_mlp_w3"],
                     mod, scr, out)


def kernel(**inputs):
    import numpy as _np
    import concourse.bacc as _bacc
    from concourse import mybir as _mybir
    from concourse.bass_utils import run_bass_kernel_spmd as _run

    nc = _bacc.Bacc("TRN2", target_bir_lowering=False, num_devices=1)
    arrays, args = {}, {}
    for name, value in inputs.items():
        v = _np.ascontiguousarray(value)
        arrays[f"in_{name}"] = v
        args[name] = nc.dram_tensor(f"in_{name}", v.shape, _mybir.dt.from_np(v.dtype), kind="ExternalInput").ap()
    out = nc.dram_tensor("out", (BATCH, SEQ, DM), fp32, kind="ExternalOutput").ap()
    build(nc, args, out)
    r = _run(nc, [arrays], core_ids=[0])
    return r.results[0]["out"]
```
